# Optimizing a Trainium2 kernel written in Bass

```python
import numpy as np
import jax
import jax.numpy as jnp

def _softmax(x, axis=-1):
    return jax.nn.softmax(x, axis=axis)

def _gelu(x):
    return jax.nn.gelu(x, approximate=True)

def _silu(x):
    return jax.nn.silu(x)

def _sigmoid(x):
    return jax.nn.sigmoid(x)

def _layernorm(x, axis=-1, eps=1e-05):
    m = jnp.mean(x, axis=axis, keepdims=True)
    v = jnp.var(x, axis=axis, keepdims=True)
    return (x - m) / jnp.sqrt(v + eps)

def _scatter_add(tgt, idx, src, axis=0):
    return tgt.at[idx].add(src)

def _segment_sum(src, seg, n):
    return jax.ops.segment_sum(src, seg, n)
kernel_name = 'mk_gnn_preln_d2_gnn_r8_b4b69a'

def setup_inputs(seed: int=0):
    np.random.seed(seed)
    _w = jnp.asarray

    def _rec_inputs():
        import jax
        import jax.numpy as jnp
        _gk = jax.random.key(seed)
        x = -8.776e-05 + 1 * jax.random.normal(jax.random.fold_in(_gk, 1), (12500, 128), jnp.float32)
        src = jax.random.randint(jax.random.fold_in(_gk, 2), (200000,), 0, 12500, jnp.int32)
        dst = jax.random.randint(jax.random.fold_in(_gk, 3), (200000,), 0, 12500, jnp.int32)
        _o = jnp.argsort(dst, stable=True)
        src = src[_o]
        dst = dst[_o]
        edge_type_460 = jax.random.randint(jax.random.fold_in(_gk, 13), (200000,), 0, 460, jnp.int32)
        return (x, src, dst, edge_type_460)
    x, src, dst, edge_type_460 = _rec_inputs()

    def _L0_gnn_setup():
        import jax, jax.numpy as jnp
        import numpy as np
        N_NODES = 5000
        N_EDGES = 80000
        D = 128
        key = jax.random.key(seed)
        ks = jax.random.split(key, 8)
        s = 1.0 / np.sqrt(D)
        x = jax.random.normal(ks[0], (N_NODES, D), dtype=jnp.float32)
        edge_index = jax.random.randint(ks[1], (2, N_EDGES), 0, N_NODES, dtype=jnp.int64)
        Wn_w = jax.random.uniform(ks[2], (D, D), jnp.float32, -s, s)
        Wn_b = jax.random.uniform(ks[3], (D,), jnp.float32, -s, s)
        Wg_w = jax.random.uniform(ks[4], (D, D), jnp.float32, -s, s)
        Wg_b = jax.random.uniform(ks[5], (D,), jnp.float32, -s, s)
        Wa_w = jax.random.uniform(ks[6], (D, D), jnp.float32, -s, s)
        Wa_b = jax.random.uniform(ks[7], (D,), jnp.float32, -s, s)
        return {'x': x, 'edge_index': edge_index, 'Wn_w': Wn_w, 'Wn_b': Wn_b, 'Wg_w': Wg_w, 'Wg_b': Wg_b, 'Wa_w': Wa_w, 'Wa_b': Wa_b}
    _L0_gnn_all = _L0_gnn_setup()
    _L0_gnn_in = {k: v for k, v in _L0_gnn_all.items() if k in ('Wn_w', 'Wn_b', 'Wg_w', 'Wg_b', 'Wa_w', 'Wa_b')}
    del _L0_gnn_all

    def _L1_gnn_setup():
        import jax, jax.numpy as jnp
        import numpy as np
        N_NODES, N_EDGES, D, N_RELS = (6250, 75000, 128, 460)
        key = jax.random.key(seed)
        ks = jax.random.split(key, 8)
        h = jax.random.normal(ks[0], (N_NODES, D), dtype=jnp.float32)
        emb_rel = jax.random.normal(ks[1], (N_RELS, D), dtype=jnp.float32)
        attn_fc_w = jax.random.normal(ks[2], (D, 3 * D), dtype=jnp.float32) * 0.05
        attn_fc2_w = jax.random.normal(ks[3], (1, D), dtype=jnp.float32) * 0.05
        loop_weight = jax.random.normal(ks[4], (D, D), dtype=jnp.float32) * 0.05
        edge_src = jax.random.randint(ks[5], (N_EDGES,), 0, N_NODES)
        edge_dst = jax.random.randint(ks[6], (N_EDGES,), 0, N_NODES)
        edge_type = jax.random.randint(ks[7], (N_EDGES,), 0, N_RELS)
        return {'h': h, 'emb_rel': emb_rel, 'attn_fc_w': attn_fc_w, 'attn_fc2_w': attn_fc2_w, 'loop_weight': loop_weight, 'edge_src': edge_src, 'edge_dst': edge_dst, 'edge_type': edge_type}
    _L1_gnn_all = _L1_gnn_setup()
    _L1_gnn_in = {k: v for k, v in _L1_gnn_all.items() if k in ('emb_rel', 'attn_fc_w', 'attn_fc2_w', 'loop_weight')}
    del _L1_gnn_all
    return {'x': x, 'src': src, 'dst': dst, 'edge_type_460': edge_type_460, 'L0_gnn_Wn_w': _L0_gnn_in['Wn_w'], 'L0_gnn_Wn_b': _L0_gnn_in['Wn_b'], 'L0_gnn_Wg_w': _L0_gnn_in['Wg_w'], 'L0_gnn_Wg_b': _L0_gnn_in['Wg_b'], 'L0_gnn_Wa_w': _L0_gnn_in['Wa_w'], 'L0_gnn_Wa_b': _L0_gnn_in['Wa_b'], 'L1_gnn_emb_rel': _L1_gnn_in['emb_rel'], 'L1_gnn_attn_fc_w': _L1_gnn_in['attn_fc_w'], 'L1_gnn_attn_fc2_w': _L1_gnn_in['attn_fc2_w'], 'L1_gnn_loop_weight': _L1_gnn_in['loop_weight']}

def reference(x, src, dst, edge_type_460, L0_gnn_Wn_w, L0_gnn_Wn_b, L0_gnn_Wg_w, L0_gnn_Wg_b, L0_gnn_Wa_w, L0_gnn_Wa_b, L1_gnn_emb_rel, L1_gnn_attn_fc_w, L1_gnn_attn_fc2_w, L1_gnn_loop_weight):
    import jax
    import jax.numpy as jnp

    def _L0_gnn_ref(x, edge_index, Wn_w, Wn_b, Wg_w, Wg_b, Wa_w, Wa_b):
        import jax, jax.numpy as jnp
        import numpy as np
        N_NODES = 5000
        N_EDGES = 80000
        D = 128
        row, col = (edge_index[0], edge_index[1])
        x_col = x[col]
        alpha = jax.nn.sigmoid(x_col @ Wa_w + Wa_b)
        neigh = x_col * alpha
        aggr = jax.ops.segment_sum(neigh, row, num_segments=x.shape[0])
        out = jnp.tanh(x @ Wn_w + Wn_b + (aggr @ Wg_w + Wg_b))
        return out

    def _L1_gnn_ref(h, emb_rel, attn_fc_w, attn_fc2_w, loop_weight, edge_src, edge_dst, edge_type):
        import jax, jax.numpy as jnp
        import numpy as np
        N_NODES, N_EDGES, D, N_RELS = (6250, 75000, 128, 460)
        n = h.shape[0]
        hs = h[edge_src]
        ht = h[edge_dst]
        rel = emb_rel[edge_type]
        z2 = jnp.concatenate([hs, ht, rel], axis=1)
        a = z2 @ attn_fc_w.T
        e = jax.nn.leaky_relu(a @ attn_fc2_w.T)
        m = jax.ops.segment_max(e, edge_dst, num_segments=n)
        m = jnp.where(jnp.isfinite(m), m, jnp.float32(0.0))
        ex = jnp.exp(e - m[edge_dst])
        den = jax.ops.segment_sum(ex, edge_dst, num_segments=n)
        alpha = ex / den[edge_dst]
        node_repr = jax.ops.segment_sum(alpha * hs, edge_dst, num_segments=n)
        node_repr = node_repr + h @ loop_weight
        return node_repr
    edge_index = jnp.stack([src, dst])
    h = jnp.maximum(_layernorm(x, axis=-1), 0.0)
    x = x + _L0_gnn_ref(h, edge_index, L0_gnn_Wn_w, L0_gnn_Wn_b, L0_gnn_Wg_w, L0_gnn_Wg_b, L0_gnn_Wa_w, L0_gnn_Wa_b)
    h = jnp.maximum(_layernorm(x, axis=-1), 0.0)
    x = x + _L1_gnn_ref(h, L1_gnn_emb_rel, L1_gnn_attn_fc_w, L1_gnn_attn_fc2_w, L1_gnn_loop_weight, src, dst, edge_type_460)
    return x

_drawn_inputs = setup_inputs


def setup_inputs(seed=0):
    import zlib

    import numpy as np

    out = dict(_drawn_inputs(seed))
    spreads = {}
    factors = {'L0_gnn_Wn_b': 2.74,
     'L0_gnn_Wg_b': 2.674,
     'L0_gnn_Wa_b': 2.875,
     'L1_gnn_emb_rel': 2.955,
     'L1_gnn_attn_fc2_w': 3.439}
    for name, (base, spread) in spreads.items():
        noise = np.random.default_rng([zlib.crc32(name.encode()), seed]).standard_normal(out[name].shape)
        drawn = base * np.exp(spread * noise) if base else spread * noise
        out[name] = jnp.asarray(drawn.astype(out[name].dtype))
    for name, factor in factors.items():
        out[name] = (out[name] * factor).astype(out[name].dtype)
    return out
```

```python
from contextlib import ExitStack

import concourse.bass as bass
from concourse import mybir

F32 = mybir.dt.float32
BF16 = mybir.dt.bfloat16
I32 = mybir.dt.int32
ALU = mybir.AluOpType
ACT = mybir.ActivationFunctionType
AX = mybir.AxisListType.X

P = 128
NODES, D = 12500, 128
EDGES = 200000
RELS = 460
TILES = -(-NODES // P)
NODES_P = TILES * P
PAD_NODE = NODES_P - 1
CHUNKS = -(-EDGES // P)
BLOCKS = -(-(CHUNKS + TILES) // P)
ROWS = BLOCKS * P
ITEMS = ROWS
TABLE = NODES_P + P
TABLES = 4
G = 7
GROUPS = TILES // G
EPS = 1e-5
SLOPE = 0.01
LOW = -1e30
RELTILES = -(-RELS // P)
ZC = 16
ZSTEPS = -(-CHUNKS // ZC)
SCAN = CHUNKS


def wait(eng, sem, value):
    if isinstance(value, int) and value <= 0:
        return
    eng.wait_ge(sem, value)


def repeat(eng, count, step):
    step(0)
    with eng.Fori(1, count) as i:
        step(i)


class Core:

    def __init__(self, nc, ctx):
        self.nc, self.ctx = nc, ctx

    def sb(self, name, shape, dt=F32):
        return self.ctx.enter_context(self.nc.sbuf_tensor(name, shape, dt))

    def ps(self, name, shape, dt=F32):
        return self.ctx.enter_context(self.nc.psum_tensor(name, shape, dt))

    def sem(self, name):
        return self.ctx.enter_context(self.nc.semaphore(name))


def group(ap, g):
    return ap[g] if isinstance(g, int) else ap[bass.ds(g, 1)].squeeze(0)


def bc(ap, shape):
    return ap.to_broadcast(shape)


def stage_constants(nc, k):
    with ExitStack() as ctx:
        c = Core(nc, ctx)
        zeroed, made = c.sem("c_zeroed"), c.sem("c_made")
        ramp = c.sb("c_ramp", [P, P], I32)
        part = c.sb("c_part", [P, 1], I32)
        block = ctx.enter_context(nc.Block())

        @block.gpsimd
        def _(pool):
            pool.memset(k.ident[:], 0.0).then_inc(zeroed, 1)
            pool.memset(k.lower[:], 1.0).then_inc(zeroed, 1)
            pool.iota(ramp[:], [[1, P]], base=0, channel_multiplier=0).then_inc(zeroed, 1)
            pool.iota(part[:], [[1, 1]], base=0, channel_multiplier=1).then_inc(zeroed, 1)
            pool.wait_ge(zeroed, 4)
            pool.affine_select(out=k.ident[:], in_=k.ident[:], compare_op=ALU.not_equal, fill=1.0,
                               base=0, pattern=[[-1, P]], channel_multiplier=1).then_inc(made, 1)
            pool.affine_select(out=k.lower[:], in_=k.lower[:], compare_op=ALU.is_gt, fill=0.0,
                               base=0, pattern=[[-1, P]], channel_multiplier=1).then_inc(made, 1)

        @block.vector
        def _(dve):
            dve.memset(k.ones[:], 1.0)
            dve.wait_ge(zeroed, 4)
            dve.tensor_copy(k.iota[:], ramp[:])
            dve.tensor_copy(k.iota_p[:], part[:])
            dve.wait_ge(made, 2)


def stage_edges(nc, k, src, dst, typ):
    with ExitStack() as ctx:
        c = Core(nc, ctx)
        raw = c.sb("e_raw", [P, 3, BLOCKS, P], I32)
        high = c.sb("e_high", [P, 3, BLOCKS, P], I32)
        highb = c.sb("e_highb", [P, 3, BLOCKS, P], BF16)
        rows = c.sb("e_rows", [P, 2, BLOCKS, P])
        turn = c.sb("e_turn", [P, 5, BLOCKS, P])
        item = c.sb("e_item", [P, 2, BLOCKS, P])
        mask = c.sb("e_mask", [P, BLOCKS, P])
        spare = c.sb("e_spare", [P, P])
        first_tile = c.sb("e_first", [P, BLOCKS])
        below = c.sb("e_below", [P, TILES, BLOCKS])
        below2 = c.sb("e_below2", [P, BLOCKS, TILES])
        count = c.sb("e_count", [P, TILES])
        last = c.sb("e_last", [P, TILES])
        item_no_i = c.sb("e_item_no_i", [P, BLOCKS], I32)
        item_no = c.sb("e_item_no", [P, BLOCKS])
        tile_of = c.sb("e_tile", [P, BLOCKS])
        tile_node = c.sb("e_tile_node", [P, BLOCKS])
        tile_rows = c.sb("e_tile_rows", [BLOCKS, P], I32)
        totals = c.ps("e_totals", [P, 512])
        turned = c.ps("e_turned", [P, 6, 4, P])
        ready, loaded, made, stored = c.sem("e_ready"), c.sem("e_loaded"), c.sem("e_made"), c.sem("e_stored")
        counted, walked, gathered, masked = c.sem("e_counted"), c.sem("e_walked"), c.sem("e_gathered"), c.sem("e_masked")
        done, copied, kept, numbered = c.sem("e_done"), c.sem("e_copied"), c.sem("e_kept"), c.sem("e_numbered")
        tiles_out, tiles_in = c.sem("e_tiles_out"), c.sem("e_tiles_in")
        block = ctx.enter_context(nc.Block())
        full = EDGES // (P * P)
        whole = EDGES // P - full * P
        rest = EDGES % P

        @block.sync
        def _(sp):
            sp.wait_ge(ready, 3)
            for n, a in enumerate((src, dst, typ)):
                at = full * P * P
                sp.dma_start(raw[:, n, 0:full, :],
                             a[0:at].rearrange("(b p f) -> p b f", p=P, f=P)).then_inc(loaded, 16)
                sp.dma_start(raw[0:whole, n, full, :],
                             a[at:at + whole * P].rearrange("(p f) -> p f", f=P)).then_inc(loaded, 16)
                sp.dma_start(raw[whole:whole + 1, n, full, 0:rest],
                             a[at + whole * P:EDGES].rearrange("(p f) -> p f", p=1)).then_inc(loaded, 16)
            sp.wait_ge(made, 1)
            for n, d in enumerate((k.src_d, k.dst_d)):
                sp.dma_start(d.rearrange("(b p) f -> p b f", p=P), rows[:, n]).then_inc(stored, 16)
            sp.wait_ge(made, 4)
            for n in range(3):
                sp.dma_start(k.high_d[n].rearrange("(b p) f -> p b f", p=P), highb[:, n]).then_inc(kept, 16)
            sp.wait_ge(masked, 5)
            sp.dma_start(k.item_src_d.rearrange("(b p) f -> p b f", p=P), turn[:, 3]).then_inc(kept, 16)
            sp.wait_ge(copied, 1)
            sp.dma_start(k.tile_d.rearrange("(b p) -> b p", p=P), tile_rows[:]).then_inc(tiles_out, 16)
            sp.wait_ge(tiles_out, 16)
            sp.dma_start(k.tile_row[:], k.tile_d.rearrange("(a p) -> a p", a=1)).then_inc(tiles_in, 16)
            sp.wait_ge(tiles_in, 16)
            sp.wait_ge(kept, 64)

        @block.gpsimd
        def _(pool):
            pool.iota(item_no_i[:], [[P, BLOCKS]], base=0, channel_multiplier=1).then_inc(numbered, 1)
            pool.wait_ge(stored, 32)
            pool.wait_ge(walked, 5)
            for b in range(BLOCKS):
                for n, d in enumerate((k.src_d, k.dst_d)):
                    pool.indirect_dma_start(item[:, n, b, :], None, d[:],
                                            bass.IndirectOffsetOnAxis(k.chunk_of[:, b:b + 1], 0)
                                            ).then_inc(gathered, 16)

        @block.vector
        def _(dve):
            for n, pad in enumerate((PAD_NODE, PAD_NODE, 0)):
                dve.memset(raw[:, n, full, :], pad).then_inc(ready, 1)
            dve.tensor_scalar(spare[:], k.iota[:], float(NODES_P), None, ALU.add).then_inc(ready, 1)
            dve.wait_ge(loaded, 16 * 9)
            dve.tensor_copy(rows[:], raw[:, 0:2]).then_inc(made, 1)
            dve.tensor_scalar(high[:], raw[:], 7, None, ALU.arith_shift_right).then_inc(made, 1)
            dve.wait_ge(made, 2)
            dve.tensor_scalar(raw[:], raw[:], P - 1, None, ALU.bitwise_and).then_inc(made, 1)
            dve.tensor_copy(highb[:], high[:]).then_inc(made, 1)
            dve.wait_ge(made, 3)
            dve.tensor_copy(turn[:, 0:3], raw[:]).then_inc(made, 1)
            dve.tensor_copy(first_tile[:], high[:, 1, :, 0]).then_inc(made, 1)
            dve.wait_ge(made, 6)
            dve.tensor_tensor(below[:], bc(first_tile[:].unsqueeze(1), [P, TILES, BLOCKS]),
                              bc(k.iota[:, 0:TILES].unsqueeze(2), [P, TILES, BLOCKS]), ALU.is_le).then_inc(made, 1)
            dve.wait_ge(made, 7)
            dve.tensor_reduce(count[:], below[:], AX, ALU.add).then_inc(made, 1)
            dve.wait_ge(counted, 1)
            dve.tensor_scalar(last[:], totals[:, 0:TILES], 1.0, float(CHUNKS), ALU.max, ALU.min).then_inc(walked, 1)
            dve.wait_ge(numbered, 1)
            dve.tensor_copy(item_no[:], item_no_i[:]).then_inc(walked, 1)
            dve.wait_ge(walked, 2)
            dve.tensor_tensor(last[:], last[:], k.iota[:, 0:TILES], ALU.add).then_inc(made, 1)
            dve.wait_ge(made, 9)
            dve.tensor_tensor(below2[:], bc(last[:].unsqueeze(1), [P, BLOCKS, TILES]),
                              bc(item_no[:].unsqueeze(2), [P, BLOCKS, TILES]), ALU.is_le).then_inc(made, 1)
            dve.wait_ge(made, 10)
            dve.tensor_reduce(tile_of[:], below2[:], AX, ALU.add).then_inc(made, 1)
            dve.wait_ge(made, 11)
            dve.tensor_scalar(tile_of[:], tile_of[:], float(TILES - 1), None, ALU.min).then_inc(walked, 1)
            dve.wait_ge(walked, 3)
            dve.tensor_scalar(tile_node[:], tile_of[:], float(P), None, ALU.mult).then_inc(walked, 1)
            dve.tensor_tensor(k.chunk_of[:], item_no[:], tile_of[:], ALU.subtract).then_inc(walked, 1)
            dve.wait_ge(walked, 5)
            dve.wait_ge(gathered, 16 * 2 * BLOCKS)
            dve.tensor_tensor(turn[:, 4], item[:, 1], bc(tile_node[:].unsqueeze(2), [P, BLOCKS, P]),
                              ALU.subtract).then_inc(masked, 1)
            dve.wait_ge(masked, 1)
            dve.tensor_scalar(mask[:], turn[:, 4], 0.0, None, ALU.is_ge).then_inc(masked, 1)
            dve.wait_ge(masked, 2)
            dve.scalar_tensor_tensor(mask[:], turn[:, 4], float(P), mask[:], ALU.is_lt, ALU.mult).then_inc(masked, 1)
            wide = bc(spare[:].unsqueeze(1), [P, BLOCKS, P])
            dve.tensor_tensor(item[:, 0], item[:, 0], wide, ALU.subtract).then_inc(made, 1)
            dve.wait_ge(masked, 3)
            dve.wait_ge(made, 12)
            dve.tensor_tensor(item[:, 0], item[:, 0], mask[:], ALU.mult).then_inc(masked, 1)
            dve.wait_ge(masked, 4)
            dve.tensor_tensor(turn[:, 3], item[:, 0], wide, ALU.add).then_inc(masked, 1)

        quads = [(n, b) for n in range(5) for b in range(0, BLOCKS, 4)]

        @block.tensor
        def _(pe):
            pe.wait_ge(made, 8)
            pe.matmul(totals[:, 0:TILES], k.ones[:], count[:], start=True, stop=True).then_inc(counted, 1)
            pe.wait_ge(walked, 3)
            pe.transpose(totals[0:BLOCKS, P:2 * P], tile_of[:], k.ident[:]).then_inc(counted, 1)
            for q, (n, b0) in enumerate(quads):
                if n == 3:
                    pe.wait_ge(masked, 5)
                if q >= 6:
                    pe.wait_ge(done, q - 5)
                for b in range(b0, min(b0 + 4, BLOCKS)):
                    mm = pe.transpose(turned[:, q % 6, b - b0, :], turn[:, n, b, :], k.ident[:])
                mm.then_inc(counted, 1)

        @block.scalar
        def _(act):
            act.wait_ge(counted, 2)
            act.copy(tile_rows[:], totals[0:BLOCKS, P:2 * P]).then_inc(copied, 1)
            for q, (n, b0) in enumerate(quads):
                act.wait_ge(counted, q + 3)
                m = min(4, BLOCKS - b0)
                act.copy(k.cols[:, n, b0 * P:(b0 + m) * P], turned[:, q % 6, 0:m, :]).then_inc(done, 1)


def stage_nodes0(nc, k, x, w):
    with ExitStack() as ctx:
        c = Core(nc, ctx)
        weights = c.sb("n_weights", [P, 2, D])
        biases = c.sb("n_biases", [2, 2, D])
        xg = c.sb("n_x", [P, 2, G, D])
        xc = c.sb("n_xc", [P, G, D])
        sq = c.sb("n_sq", [P, G, D])
        h = c.sb("n_h", [P, 2, G, D])
        hT = c.sb("n_hT", [P, G, P])
        sig = c.sb("n_sig", [P, G, D])
        pre = c.sb("n_pre", [P, 2, G, D])
        sums = c.sb("n_sums", [P, 4, G])
        psT = c.ps("n_psT", [P, 8, P])
        psM = c.ps("n_psM", [P, 8, 2, D])
        pad = c.sb("n_pad", [P, D])
        zero = c.sb("n_zero", [P, D])
        padded, copied, wts, out = c.sem("n_padded"), c.sem("n_copied"), c.sem("n_wts"), [c.sem("n_out0"), c.sem("n_out1")]
        x_in = [c.sem("n_x_in0"), c.sem("n_x_in1")]
        centred, link, rooted, hs, turned, copies = (c.sem("n_" + s) for s in ("centred", "link", "rooted", "hs", "turned", "copies"))
        mult, sigs, pres, us = (c.sem("n_" + s) for s in ("mult", "sigs", "pres", "us"))
        zeroed, tables = c.sem("n_zeroed"), c.sem("n_tables")
        block = ctx.enter_context(nc.Block())
        xv = k.x_d.rearrange("(g t p) d -> g p t d", p=P, t=G)
        prev = k.pre_d.rearrange("(g t p) d -> g p t d", p=P, t=G)
        LINKS = 5

        @block.sync
        def _(sp):
            for n, name in enumerate(("L0_gnn_Wa_w", "L0_gnn_Wn_w")):
                sp.dma_start(weights[:, n, :], w[name]).then_inc(wts, 16)
            sp.wait_ge(zeroed, 2)
            for r, n, name in ((0, 0, "L0_gnn_Wa_b"), (0, 1, "L0_gnn_Wn_b"), (1, 1, "L0_gnn_Wg_b")):
                sp.dma_start(biases[r:r + 1, n, :], w[name].rearrange("(a d) -> a d", a=1)).then_inc(wts, 16)
            sp.dma_start(k.x_d[0:NODES, :], x).then_inc(copied, 16)
            sp.dma_start(k.x_d[NODES:NODES_P, :], pad[0:NODES_P - NODES, :]).then_inc(copied, 16)
            sp.wait_ge(copied, 32)

            def step(i):
                for s in range(2):
                    g = 2 * i + s
                    wait(sp, us, g - 1)
                    sp.dma_start(xg[:, s], group(xv, g)).then_inc(x_in[s], 16)
            repeat(sp, GROUPS // 2, step)

        @block.gpsimd
        def _(pool):
            pool.memset(pad[:], 0.0).then_inc(zeroed, 1)
            pool.memset(biases[:], 0.0).then_inc(zeroed, 1)
            pool.memset(zero[:], 0.0).then_inc(zeroed, 1)

        @block.vector
        def _(dve):
            def step(i):
                for s in range(2):
                    g = 2 * i + s
                    dve.wait_ge(x_in[s], 16 * (i + 1))
                    dve.tensor_reduce(sums[:, 0], xg[:, s], AX, ALU.add).then_inc(link, 1)
                    dve.wait_ge(link, LINKS * g + 1)
                    dve.tensor_scalar(sums[:, 1], sums[:, 0], -1.0 / D, None, ALU.mult).then_inc(link, 1)
                    dve.wait_ge(link, LINKS * g + 2)
                    dve.tensor_tensor(xc[:], xg[:, s], bc(sums[:, 1].unsqueeze(2), [P, G, D]), ALU.add).then_inc(link, 1)
                    dve.wait_ge(link, LINKS * g + 3)
                    dve.tensor_tensor(sq[:], xc[:], xc[:], ALU.mult).then_inc(link, 1)
                    dve.wait_ge(link, LINKS * g + 4)
                    dve.tensor_reduce(sums[:, 2], sq[:], AX, ALU.add).then_inc(link, 1)
                    dve.wait_ge(link, LINKS * g + 5)
                    dve.tensor_scalar(sums[:, 2], sums[:, 2], 1.0 / D, EPS, ALU.mult, ALU.add).then_inc(centred, 1)
                    dve.wait_ge(rooted, g + 1)
                    dve.reciprocal(sums[:, 1], sums[:, 3]).then_inc(hs, 1)
                    dve.wait_ge(hs, 2 * g + 1)
                    wait(dve, turned, g - 1)
                    dve.scalar_tensor_tensor(h[:, s], xc[:], 0.0, bc(sums[:, 1].unsqueeze(2), [P, G, D]),
                                             ALU.max, ALU.mult).then_inc(hs, 1)
                    dve.wait_ge(sigs, g + 1)
                    dve.tensor_tensor(k.u[:, bass.ds(g * G, G), :], h[:, s], sig[:], ALU.mult).then_inc(us, 1)
            repeat(dve, GROUPS // 2, step)

        @block.tensor
        def _(pe):
            pe.wait_ge(wts, 16 * 5)

            def step(i):
                for s in range(2):
                    g = 2 * i + s
                    pe.wait_ge(hs, 2 * g + 2)
                    wait(pe, copies, g)
                    for t in range(G):
                        mm = pe.transpose(psT[:, t, :], h[:, s, t, :], k.ident[:])
                    mm.then_inc(turned, 1)
                    pe.wait_ge(copies, g + 1)
                    wait(pe, pres, g)
                    wait(pe, sigs, g)
                    for t in range(G):
                        pe.matmul(psM[:, t], k.ones[0:2, :], biases[:], start=True, stop=False)
                        mm = pe.matmul(psM[:, t], hT[:, t, :], weights[:], start=False, stop=True)
                    mm.then_inc(mult, 1)
            repeat(pe, GROUPS // 2, step)

        @block.scalar
        def _(act):
            act.wait_ge(zeroed, 3)
            for t in range(TABLES):
                act.dma_start(k.table_d[t].rearrange("(t p) d -> p t d", p=P),
                              bc(zero[:].unsqueeze(1), [P, TABLE // P, D])).then_inc(tables, 16)

            def step(i):
                for s in range(2):
                    g = 2 * i + s
                    act.wait_ge(centred, g + 1)
                    act.activation(sums[:, 3], sums[:, 2], ACT.Sqrt).then_inc(rooted, 1)
                    act.wait_ge(turned, g + 1)
                    wait(act, mult, g)
                    act.copy(hT[:], psT[:, 0:G]).then_inc(copies, 1)
                    act.wait_ge(mult, g + 1)
                    wait(act, us, g)
                    act.activation(sig[:], psM[:, 0:G, 0, :], ACT.Sigmoid).then_inc(sigs, 1)
                    wait(act, out[s], 16 * i)
                    act.copy(pre[:, s], psM[:, 0:G, 1, :]).then_inc(pres, 1)
                    act.wait_ge(pres, g + 1)
                    act.dma_start(group(prev, g), pre[:, s]).then_inc(out[s], 16)
            repeat(act, GROUPS // 2, step)
            act.wait_ge(tables, 16 * TABLES)
            for s in range(2):
                act.wait_ge(out[s], 16 * (GROUPS // 2))


def stage_messages0(nc, k):
    with ExitStack() as ctx:
        c = Core(nc, ctx)
        wide = c.sb("m_wide", [P, 2, TABLES, P])
        same = c.sb("m_same", [P, 2, TABLES, P], BF16)
        member = c.sb("m_member", [P, 2, TABLES, P], BF16)
        earlier = c.sb("m_earlier", [P, TABLES, P], BF16)
        count = c.sb("m_count", [P, 4, TABLES])
        spare = c.sb("m_spare", [P, 1])
        place = c.sb("m_place", [P, 2, TABLES], I32)
        mix = c.sb("m_mix", [P, 2, TABLES, P])
        rows = c.sb("m_rows", [P, 2, TABLES, D])
        ps_mix = c.ps("m_ps_mix", [P, 2, TABLES, P])
        ps_rows = c.ps("m_ps_rows", [P, 2, TABLES, D])
        wide_in = [c.sem("m_wide_in0"), c.sem("m_wide_in1")]
        sames, members, link, places = (c.sem("m_" + s) for s in ("sames", "members", "link", "places"))
        mixed, mixes, summed, rowed = (c.sem("m_" + s) for s in ("mixed", "mixes", "summed", "rowed"))
        added = [c.sem(f"m_added{t}") for t in range(TABLES)]
        sent, turns = c.sem("m_sent"), c.sem("m_turns")
        block = ctx.enter_context(nc.Block())
        STEPS = ITEMS // TABLES // 2
        LINKS = 5
        srcs = k.item_src_d.rearrange("(g t) e -> g (t e)", t=TABLES)

        @block.sync
        def _(sp):
            def step(i):
                for s in range(2):
                    g = 2 * i + s
                    wait(sp, sames, g - 1)
                    sp.dma_start(wide[:, s].rearrange("p t e -> p (t e)"),
                                 group(srcs, g).partition_broadcast(P)).then_inc(wide_in[s], 16)
            repeat(sp, STEPS, step)

        @block.vector
        def _(dve):
            dve.tensor_scalar(spare[:], k.iota_p[:], float(NODES_P), None, ALU.add).then_inc(link, 1)

            def step(i):
                for s in range(2):
                    g = 2 * i + s
                    mine = k.cols[:, 3, bass.ds(g * TABLES, TABLES)]
                    nodes = k.cols[:, 4, bass.ds(g * TABLES, TABLES)]
                    wait(dve, mixed, g - 1)
                    dve.wait_ge(wide_in[s], 16 * (i + 1))
                    dve.tensor_tensor(same[:, s], wide[:, s], bc(mine.unsqueeze(2), [P, TABLES, P]),
                                      ALU.is_equal).then_inc(sames, 1)
                    dve.tensor_tensor(member[:, s], bc(k.iota[:].unsqueeze(1), [P, TABLES, P]),
                                      bc(nodes.unsqueeze(2), [P, TABLES, P]), ALU.is_equal).then_inc(members, 1)
                    dve.wait_ge(sames, g + 1)
                    dve.tensor_tensor(earlier[:], same[:, s], bc(k.lower[:].unsqueeze(1), [P, TABLES, P]),
                                      ALU.mult).then_inc(link, 1)
                    dve.wait_ge(link, LINKS * g + 2)
                    dve.tensor_reduce(count[:, 0], earlier[:], AX, ALU.add).then_inc(link, 1)
                    dve.tensor_scalar(count[:, 1], mine, spare[:, 0:1], None, ALU.subtract).then_inc(link, 1)
                    dve.wait_ge(link, LINKS * g + 4)
                    dve.tensor_scalar(count[:, 2], count[:, 0], 0.0, None, ALU.is_equal).then_inc(link, 1)
                    dve.wait_ge(link, LINKS * g + 5)
                    dve.tensor_tensor(count[:, 3], count[:, 1], count[:, 2], ALU.mult).then_inc(link, 1)
                    dve.wait_ge(link, LINKS * g + 6)
                    wait(dve, sent, g - 1)
                    dve.tensor_scalar(place[:, s], count[:, 3], spare[:, 0:1], None, ALU.add).then_inc(places, 1)
            repeat(dve, STEPS, step)

        @block.tensor
        def _(pe):
            def step(i):
                for s in range(2):
                    g = 2 * i + s
                    pe.wait_ge(members, g + 1)
                    wait(pe, mixes, g - 1)
                    for t in range(TABLES):
                        mm = pe.matmul(ps_mix[:, s, t, :], member[:, s, t, :], same[:, s, t, :], start=True, stop=True)
                    mm.then_inc(mixed, 1)
                    pe.wait_ge(mixes, g + 1)
                    wait(pe, rowed, g - 1)
                    for t in range(TABLES):
                        tile = pe.value_load(k.tile_row[0:1, bass.ds(g * TABLES + t, 1)], min_val=0, max_val=TILES - 1)
                        mm = pe.matmul(ps_rows[:, s, t, :], mix[:, s, t, :],
                                       k.u[:, bass.ds(tile, 1), :].squeeze(1), start=True, stop=True)
                    mm.then_inc(summed, 1)
            repeat(pe, STEPS, step)

        @block.scalar
        def _(act):
            def step(i):
                for s in range(2):
                    g = 2 * i + s
                    act.wait_ge(mixed, g + 1)
                    wait(act, summed, g - 1)
                    act.copy(mix[:, s], ps_mix[:, s]).then_inc(mixes, 1)
                    act.wait_ge(summed, g + 1)
                    wait(act, sent, g - 1)
                    act.copy(rows[:, s], ps_rows[:, s]).then_inc(rowed, 1)
            repeat(act, STEPS, step)

        @block.gpsimd
        def _(pool):
            def step(i):
                for s in range(2):
                    g = 2 * i + s
                    pool.wait_ge(places, g + 1)
                    pool.wait_ge(rowed, g + 1)
                    for t in range(TABLES):
                        wait(pool, added[t], 16 * g)
                        pool.sem_inc(turns, 1)
                        pool.indirect_dma_start(k.table_d[t], bass.IndirectOffsetOnAxis(place[:, s, t:t + 1], 0),
                                                rows[:, s, t, :], None, compute_op=ALU.add).then_inc(added[t], 16)
                    if not (isinstance(g, int) and g == 0):
                        pool.sem_inc(sent, 1)
            repeat(pool, STEPS, step)
            for t in range(TABLES):
                pool.wait_ge(added[t], 16 * ITEMS // TABLES)


def stage_weights1(nc, k, w):
    with ExitStack() as ctx:
        c = Core(nc, ctx)
        fc = c.sb("w_fc", [P, 3, D])
        fc2 = c.sb("w_fc2", [P, 1])
        emb = c.sb("w_emb", [P, RELTILES, D])
        embT = c.sb("w_embT", [P, RELTILES, P])
        rel = c.sb("w_rel", [P, RELTILES])
        vec = c.sb("w_vec", [P, 3])
        psv = c.ps("w_psv", [P, 512])
        pse = c.ps("w_pse", [P, RELTILES, P])
        psr = c.ps("w_psr", [P, 512])
        loaded, prods, taken, zeroed = (c.sem("w_" + s) for s in ("loaded", "prods", "taken", "zeroed"))
        block = ctx.enter_context(nc.Block())

        @block.sync
        def _(sp):
            sp.dma_start(fc[:], w["L1_gnn_attn_fc_w"].rearrange("o (n i) -> o n i", n=3)).then_inc(loaded, 16)
            sp.dma_start(fc2[:], w["L1_gnn_attn_fc2_w"].rearrange("a o -> o a")).then_inc(loaded, 16)
            sp.dma_start(k.w1[:, 0:D], w["L1_gnn_loop_weight"]).then_inc(loaded, 16)
            sp.dma_start(k.wg[:], w["L0_gnn_Wg_w"]).then_inc(loaded, 16)
            sp.wait_ge(zeroed, 1)
            full = RELS // P
            sp.dma_start(emb[:, 0:full, :], w["L1_gnn_emb_rel"][0:full * P, :].rearrange("(t p) d -> p t d", p=P)).then_inc(loaded, 16)
            sp.dma_start(emb[0:RELS - full * P, full, :], w["L1_gnn_emb_rel"][full * P:RELS, :]).then_inc(loaded, 16)

        @block.vector
        def _(dve):
            dve.memset(emb[:, RELS // P, :], 0.0).then_inc(zeroed, 1)
            dve.wait_ge(prods, 1)
            dve.tensor_copy(vec[:], psv[:, 0:3]).then_inc(taken, 1)
            dve.wait_ge(loaded, 16 * 6)
            dve.tensor_copy(k.w1[:, D:D + 2], psv[:, 0:2]).then_inc(taken, 1)
            dve.wait_ge(prods, 2)
            dve.tensor_copy(embT[:], pse[:]).then_inc(taken, 1)
            dve.wait_ge(prods, 3)
            dve.tensor_copy(rel[:], psr[:, 0:RELTILES]).then_inc(taken, 1)
            dve.wait_ge(prods, 4)
            split3(dve, taken, 4, k.parts[0:RELTILES, 2], k.split[0:RELTILES, 2], psr[0:RELTILES, P:2 * P])

        @block.tensor
        def _(pe):
            pe.wait_ge(loaded, 16 * 6)
            for n in range(3):
                mm = pe.matmul(psv[:, n:n + 1], fc[:, n, :], fc2[:], start=True, stop=True)
            mm.then_inc(prods, 1)
            for t in range(RELTILES):
                mm = pe.transpose(pse[:, t, :], emb[:, t, :], k.ident[:])
            mm.then_inc(prods, 1)
            pe.wait_ge(taken, 3)
            for t in range(RELTILES):
                mm = pe.matmul(psr[:, t:t + 1], embT[:, t, :], vec[:, 2:3], start=True, stop=True)
            mm.then_inc(prods, 1)
            pe.wait_ge(taken, 4)
            pe.transpose(psr[0:RELTILES, P:2 * P], rel[:], k.ident[:]).then_inc(prods, 1)


def split3(dve, link, base, parts, left, whole):
    dve.tensor_copy(parts[:, 0, :], whole).then_inc(link, 1)
    dve.wait_ge(link, base + 1)
    dve.tensor_tensor(left[:, 0, :], whole, parts[:, 0, :], ALU.subtract).then_inc(link, 1)
    dve.wait_ge(link, base + 2)
    dve.tensor_copy(parts[:, 1, :], left[:, 0, :]).then_inc(link, 1)
    dve.wait_ge(link, base + 3)
    dve.tensor_tensor(left[:, 1, :], left[:, 0, :], parts[:, 1, :], ALU.subtract).then_inc(link, 1)
    dve.wait_ge(link, base + 4)
    dve.tensor_copy(parts[:, 2, :], left[:, 1, :]).then_inc(link, 1)


def stage_nodes1(nc, k):
    with ExitStack() as ctx:
        c = Core(nc, ctx)
        xg = c.sb("p_x", [P, 2, G, D])
        pre = c.sb("p_pre", [P, 2, G, D])
        parts = c.sb("p_parts", [P, 2, TABLES, G, D])
        agg = c.sb("p_agg", [P, 2, G, D])
        x1 = c.sb("p_x1", [P, G, D])
        xc = c.sb("p_xc", [P, G, D])
        sq = c.sb("p_sq", [P, G, D])
        h = c.sb("p_h", [P, 2, G, D])
        gate = c.sb("p_gate", [P, G, D])
        aT = c.sb("p_aT", [P, G, P])
        hT = c.sb("p_hT", [P, G, P])
        basis = c.sb("p_basis", [P, 2, G, D])
        sums = c.sb("p_sums", [P, 4, G])
        psT = c.ps("p_psT", [P, 8, P])
        psG = c.ps("p_psG", [P, 8, P])
        psL = c.ps("p_psL", [P, 3, 512])
        x_in = [c.sem("p_x_in0"), c.sem("p_x_in1")]
        link, summed, turned, copied, mult, gates = (c.sem("p_" + s) for s in ("link", "summed", "turned", "copied", "mult", "gates"))
        centred, rooted, hs, looped, basics, moved = (c.sem("p_" + s) for s in ("centred", "rooted", "hs", "looped", "basics", "moved"))
        h_out = [c.sem("p_h_out0"), c.sem("p_h_out1")]
        b_out = [c.sem("p_b_out0"), c.sem("p_b_out1")]
        block = ctx.enter_context(nc.Block())
        view = lambda d: d.rearrange("(g t p) d -> g p t d", p=P, t=G)
        xv, prev, hv, bv = view(k.x_d), view(k.pre_d), view(k.h1_d), view(k.basis_d)
        tv = [view(k.table_d[t][0:NODES_P, :]) for t in range(TABLES)]
        LINKS = 9

        @block.sync
        def _(sp):
            def step(i):
                for s in range(2):
                    g = 2 * i + s
                    wait(sp, moved, g - 1)
                    for t in range(TABLES):
                        sp.dma_start(parts[:, s, t], group(tv[t], g)).then_inc(x_in[s], 16)
                    sp.dma_start(pre[:, s], group(prev, g)).then_inc(x_in[s], 16)
                    sp.dma_start(xg[:, s], group(xv, g)).then_inc(x_in[s], 16)
            repeat(sp, GROUPS // 2, step)

        @block.vector
        def _(dve):
            def step(i):
                for s in range(2):
                    g = 2 * i + s
                    dve.wait_ge(x_in[s], 16 * 6 * (i + 1))
                    dve.tensor_tensor(parts[:, s, 0:2], parts[:, s, 0:2], parts[:, s, 2:4], ALU.add).then_inc(link, 1)
                    dve.wait_ge(link, LINKS * g + 1)
                    wait(dve, turned, 2 * g - 2)
                    dve.tensor_tensor(agg[:, s], parts[:, s, 0], parts[:, s, 1], ALU.add).then_inc(summed, 1)
                    dve.wait_ge(mult, g + 1)
                    dve.tensor_tensor(xc[:], psG[:, 0:G], pre[:, s], ALU.add).then_inc(link, 1)
                    dve.wait_ge(gates, g + 1)
                    dve.tensor_tensor(x1[:], gate[:], xg[:, s], ALU.add).then_inc(link, 1)
                    dve.wait_ge(link, LINKS * g + 3)
                    dve.tensor_reduce(sums[:, 0], x1[:], AX, ALU.add).then_inc(link, 1)
                    dve.wait_ge(link, LINKS * g + 4)
                    dve.tensor_scalar(sums[:, 1], sums[:, 0], -1.0 / D, None, ALU.mult).then_inc(link, 1)
                    dve.wait_ge(link, LINKS * g + 5)
                    dve.tensor_tensor(xc[:], x1[:], bc(sums[:, 1].unsqueeze(2), [P, G, D]), ALU.add).then_inc(link, 1)
                    dve.wait_ge(link, LINKS * g + 6)
                    dve.tensor_tensor(sq[:], xc[:], xc[:], ALU.mult).then_inc(link, 1)
                    dve.wait_ge(link, LINKS * g + 7)
                    dve.tensor_reduce(sums[:, 2], sq[:], AX, ALU.add).then_inc(link, 1)
                    dve.wait_ge(link, LINKS * g + 8)
                    dve.tensor_scalar(sums[:, 2], sums[:, 2], 1.0 / D, EPS, ALU.mult, ALU.add).then_inc(centred, 1)
                    dve.wait_ge(rooted, g + 1)
                    dve.reciprocal(sums[:, 1], sums[:, 3]).then_inc(link, 1)
                    dve.wait_ge(link, LINKS * g + 9)
                    wait(dve, turned, 2 * g - 2)
                    wait(dve, h_out[s], 16 * i)
                    dve.scalar_tensor_tensor(h[:, s], xc[:], 0.0, bc(sums[:, 1].unsqueeze(2), [P, G, D]),
                                             ALU.max, ALU.mult).then_inc(hs, 1)
                    dve.wait_ge(looped, g + 1)
                    wait(dve, b_out[s], 16 * i)
                    for a, n in ((0, 3), (3, 3), (6, 1)):
                        part = psL[:, a // 3, 0:n * (D + 2)].rearrange("p (t d) -> p t d", t=n)
                        dve.tensor_tensor(basis[:, s, a:a + n], x1[:, a:a + n], part[:, :, 0:D], ALU.add).then_inc(basics, 1)
                        for m in range(2):
                            mv = dve.tensor_copy(k.node_scores[:, m, bass.ds(g * G + a, n)], part[:, :, D + m])
                    mv.then_inc(moved, 1)
            repeat(dve, GROUPS // 2, step)

        @block.tensor
        def _(pe):
            def step(i):
                for s in range(2):
                    g = 2 * i + s
                    pe.wait_ge(summed, g + 1)
                    wait(pe, copied, 2 * g)
                    for t in range(G):
                        mm = pe.transpose(psT[:, t, :], agg[:, s, t, :], k.ident[:])
                    mm.then_inc(turned, 1)
                    pe.wait_ge(copied, 2 * g + 1)
                    for t in range(G):
                        mm = pe.matmul(psG[:, t, :], aT[:, t, :], k.wg[:], start=True, stop=True)
                    mm.then_inc(mult, 1)
                    pe.wait_ge(hs, g + 1)
                    for t in range(G):
                        mm = pe.transpose(psT[:, t, :], h[:, s, t, :], k.ident[:])
                    mm.then_inc(turned, 1)
                    pe.wait_ge(copied, 2 * g + 2)
                    wait(pe, moved, g)
                    for t in range(G):
                        at = (t % 3) * (D + 2)
                        mm = pe.matmul(psL[:, t // 3, at:at + D + 2], hT[:, t, :], k.w1[:], start=True, stop=True)
                    mm.then_inc(looped, 1)
            repeat(pe, GROUPS // 2, step)

        @block.scalar
        def _(act):
            def step(i):
                for s in range(2):
                    g = 2 * i + s
                    act.wait_ge(turned, 2 * g + 1)
                    wait(act, mult, g)
                    act.copy(aT[:], psT[:, 0:G]).then_inc(copied, 1)
                    act.wait_ge(link, LINKS * g + 2)
                    act.activation(gate[:], xc[:], ACT.Tanh).then_inc(gates, 1)
                    act.wait_ge(centred, g + 1)
                    act.activation(sums[:, 3], sums[:, 2], ACT.Sqrt).then_inc(rooted, 1)
                    act.wait_ge(hs, g + 1)
                    act.dma_start(group(hv, g), h[:, s]).then_inc(h_out[s], 16)
                    act.wait_ge(turned, 2 * g + 2)
                    wait(act, looped, g)
                    act.copy(hT[:], psT[:, 0:G]).then_inc(copied, 1)
                    act.wait_ge(basics, 3 * g + 3)
                    act.dma_start(group(bv, g), basis[:, s]).then_inc(b_out[s], 16)
            repeat(act, GROUPS // 2, step)
            for s in range(2):
                act.wait_ge(h_out[s], 16 * (GROUPS // 2))
                act.wait_ge(b_out[s], 16 * (GROUPS // 2))


def stage_scores(nc, k):
    with ExitStack() as ctx:
        c = Core(nc, ctx)
        wide = c.sb("z_wide", [P, 2, 3, ZC * P], BF16)
        pick = c.sb("z_pick", [P, 2, 3, ZC * P], BF16)
        junk = c.sb("z_junk", [P, 12, P])
        z3 = c.sb("z_z3", [P, 3, ROWS])
        psT = c.ps("z_psT", [P, 2, 512])
        psZ = c.ps("z_psZ", [P, 6, 512])
        wide_in = [c.sem("z_wide_in0"), c.sem("z_wide_in1")]
        turned, link, picks, looked, zs, summed = (c.sem("z_" + s) for s in ("turned", "link", "picks", "looked", "zs", "summed"))
        cleared, copied, out, back = (c.sem("z_" + s) for s in ("cleared", "copied", "out", "back"))
        zt = c.sb("z_zt", [P, BLOCKS, P])
        block = ctx.enter_context(nc.Block())
        highs = TILES, TILES, RELTILES
        hv = k.high_d.rearrange("n (g c) e -> g n (c e)", c=ZC)
        assert ZSTEPS % 2 == 0

        @block.sync
        def _(sp):
            def step(i):
                for s in range(2):
                    g = 2 * i + s
                    wait(sp, picks, g - 1)
                    for n in range(3):
                        sp.dma_start(wide[0:highs[n], s, n, :], group(hv, g)[n].partition_broadcast(highs[n])
                                     ).then_inc(wide_in[s], 16)
            repeat(sp, ZSTEPS // 2, step)
            sp.wait_ge(copied, -(-BLOCKS // 4))
            sp.dma_start(k.z_d.rearrange("(b p) e -> p b e", p=P), zt[:]).then_inc(out, 16)
            sp.wait_ge(out, 16)

        @block.vector
        def _(dve):
            dve.memset(z3[:, :, ZSTEPS * ZC:], 0.0).then_inc(cleared, 1)
            for n in range(2):
                dve.wait_ge(turned, n + 1)
                split3(dve, link, 5 * n, k.parts[0:TILES, n], k.split[0:TILES, n], psT[0:TILES, n, 0:P])
            dve.wait_ge(link, 10)

            def step(i):
                for s in range(2):
                    g = 2 * i + s
                    dve.wait_ge(wide_in[s], 16 * 3 * (i + 1))
                    wait(dve, looked, (g - 1) * ZC)
                    for n in range(3):
                        op = dve.tensor_scalar(pick[0:highs[n], s, n], wide[0:highs[n], s, n],
                                               k.iota_p[0:highs[n], 0:1], None, ALU.is_equal)
                    op.then_inc(picks, 1)
                    for j in range(ZC):
                        dve.wait_ge(looked, g * ZC + j + 1)
                        col = g * ZC + j
                        wait(dve, zs, col - 3)
                        for n in range(3):
                            op = dve.scalar_tensor_tensor(junk[:, (3 * j + n) % 12, :], k.iota[:], k.cols[:, n, bass.ds(col, 1)],
                                                          psZ[:, j % 6, n * P:(n + 1) * P], ALU.is_equal, ALU.mult,
                                                          accum_out=z3[:, n, bass.ds(col, 1)])
                        op.then_inc(zs, 1)
            repeat(dve, ZSTEPS // 2, step)
            dve.wait_ge(zs, ZSTEPS * ZC)
            dve.tensor_tensor(z3[:, 0], z3[:, 0], z3[:, 1], ALU.add).then_inc(summed, 1)
            dve.wait_ge(summed, 1)
            dve.tensor_tensor(z3[:, 0], z3[:, 0], z3[:, 2], ALU.add).then_inc(summed, 1)

        @block.tensor
        def _(pe):
            for n in range(2):
                pe.transpose(psT[0:TILES, n, 0:P], k.node_scores[:, n, :], k.ident[:]).then_inc(turned, 1)
            pe.wait_ge(link, 10)

            def step(i):
                for s in range(2):
                    g = 2 * i + s
                    pe.wait_ge(picks, g + 1)
                    for j in range(ZC):
                        wait(pe, zs, g * ZC + j - 5)
                        for n in range(3):
                            for m in range(3):
                                mm = pe.matmul(psZ[:, j % 6, n * P:(n + 1) * P], pick[0:highs[n], s, n, j * P:(j + 1) * P],
                                               k.parts[0:highs[n], n, m, :], start=(m == 0), stop=(m == 2))
                        mm.then_inc(looked, 1)
            repeat(pe, ZSTEPS // 2, step)
            pe.wait_ge(summed, 2)
            for q, b0 in enumerate(range(0, BLOCKS, 4)):
                if q >= 2:
                    pe.wait_ge(copied, q - 1)
                for b in range(b0, min(b0 + 4, BLOCKS)):
                    at = (b - b0) * P
                    mm = pe.transpose(psT[:, q % 2, at:at + P], z3[:, 0, b * P:(b + 1) * P], k.ident[:])
                mm.then_inc(turned, 1)

        @block.scalar
        def _(act):
            for q, b0 in enumerate(range(0, BLOCKS, 4)):
                m = min(4, BLOCKS - b0)
                act.wait_ge(turned, q + 3)
                act.copy(zt[:, b0:b0 + m, :].rearrange("p b e -> p (b e)"), psT[:, q % 2, 0:m * P]).then_inc(copied, 1)


def stage_softmax(nc, k):
    with ExitStack() as ctx:
        c = Core(nc, ctx)
        dstp = c.sb("s_dst", [P, SCAN])
        before = c.sb("s_before", [P, 1])
        after = c.sb("s_after", [P, 1])
        z = c.sb("s_z", [P, SCAN])
        cut = c.sb("s_cut", [P, SCAN + 1])
        top = c.sb("s_top", [P, SCAN])
        top2 = c.sb("s_top2", [P, SCAN])
        ends = c.sb("s_ends", [P, 2])
        rowsT = c.sb("s_rowsT", [1, 2, P])
        carry = c.sb("s_carry", [1, P + 1])
        colc = c.sb("s_colc", [P, 2])
        wts = c.sb("s_wts", [P, 2, BLOCKS, P])
        zero = c.sb("s_zero", [P, P])
        psA = c.ps("s_psA", [P, 512])
        psB = c.ps("s_psB", [P, 512])
        psW = c.ps("s_psW", [P, 4, 512])
        loaded, sent, link, turned, moved, exped = (c.sem("s_" + s) for s in ("loaded", "sent", "link", "turned", "moved", "exped"))
        out, gathered, wT, wc = (c.sem("s_" + s) for s in ("out", "gathered", "wT", "wc"))
        block = ctx.enter_context(nc.Block())
        N = P * SCAN
        flat = lambda d: d.rearrange("r e -> (r e)")
        runs = lambda d: flat(d)[0:N].rearrange("(p j) -> p j", p=P)

        @block.sync
        def _(sp):
            sp.wait_ge(sent, 3)
            sp.dma_start(dstp[:], runs(k.dst_d)).then_inc(loaded, 16)
            sp.dma_start(z[:], runs(k.z_d)).then_inc(loaded, 16)
            last = flat(k.dst_d)[SCAN - 1:N - 1].rearrange("(p j) -> p j", p=1)
            nxt = runs(k.dst_d)
            with nc.allow_non_contiguous_dma("127 single numbers"):
                sp.dma_start(before[1:P, :], nxt[0:P - 1, SCAN - 1:SCAN]).then_inc(loaded, 16)
                sp.dma_start(after[0:P - 1, :], nxt[1:P, 0:1]).then_inc(loaded, 16)
            sp.dma_start(flat(k.w_d)[N:ROWS * P].rearrange("(p j) -> p j", j=P), zero[0:ROWS - CHUNKS, :]).then_inc(out, 16)
            sp.wait_ge(exped, 1)
            sp.dma_start(runs(k.w_d), top[:]).then_inc(out, 16)

        @block.vector
        def _(dve):
            n = [0]

            def link_up(op):
                n[0] += 1
                op.then_inc(link, 1)
                dve.wait_ge(link, n[0])

            dve.memset(before[:], -1.0).then_inc(sent, 1)
            dve.memset(after[:], -1.0).then_inc(sent, 1)
            dve.memset(zero[:], 0.0).then_inc(sent, 1)
            dve.wait_ge(loaded, 64)
            link_up(dve.tensor_tensor(cut[:, 1:SCAN], dstp[:, 1:SCAN], dstp[:, 0:SCAN - 1], ALU.not_equal))
            link_up(dve.tensor_tensor(cut[:, 0:1], dstp[:, 0:1], before[:], ALU.not_equal))
            link_up(dve.tensor_tensor(cut[:, SCAN:], dstp[:, SCAN - 1:], after[:], ALU.not_equal))
            link_up(dve.tensor_scalar(cut[:], cut[:], LOW, None, ALU.mult))
            link_up(dve.scalar_tensor_tensor(z[:], z[:], SLOPE, z[:], ALU.mult, ALU.max))

            for turn in range(2):
                a = z if turn == 0 else top
                b = top if turn == 0 else top2
                data = a[:] if turn == 0 else a[:, ::-1]
                outp = b[:] if turn == 0 else b[:, ::-1]
                gaps = cut[:, 0:SCAN] if turn == 0 else cut[:, SCAN:0:-1]
                link_up(dve.tensor_tensor_scan(outp, gaps, data, LOW, ALU.add, ALU.max))
                end = b[:, SCAN - 1:SCAN] if turn == 0 else b[:, 0:1]
                link_up(dve.tensor_copy(ends[:, 0:1], end))
                link_up(dve.tensor_reduce(ends[:, 1:2], gaps, AX, ALU.min))
                dve.wait_ge(turned, turn + 1)
                link_up(dve.tensor_copy(rowsT[:, 0], psA[0:1, 0:P]))
                link_up(dve.tensor_copy(rowsT[:, 1], psA[0:1, P:2 * P]))
                link_up(dve.memset(carry[:], LOW))
                if turn == 0:
                    link_up(dve.tensor_tensor_scan(carry[:, 1:P + 1], rowsT[:, 1], rowsT[:, 0], LOW, ALU.add, ALU.max))
                    use = carry[:, 0:P]
                else:
                    link_up(dve.tensor_tensor_scan(carry[:, 0:P][:, ::-1], rowsT[:, 1][:, ::-1], rowsT[:, 0][:, ::-1],
                                                   LOW, ALU.add, ALU.max))
                    use = carry[:, 1:P + 1]
                link_up(dve.tensor_copy(rowsT[:, 0], use))
                dve.wait_ge(moved, turn + 1)
                link_up(dve.tensor_copy(colc[:, 0:1], psB[:, 0:1]))
                link_up(dve.tensor_tensor_scan(outp, gaps, data, colc[:, 0:1], ALU.add, ALU.max))
            link_up(dve.tensor_tensor(z[:], z[:], top2[:], ALU.subtract))
            for b0 in range(0, BLOCKS, 4):
                m = min(4, BLOCKS - b0)
                dve.wait_ge(wT, b0 // 4 + 1)
                dve.tensor_copy(k.wcol[:, b0 * P:(b0 + m) * P], psW[:, b0 // 4, 0:m * P]).then_inc(wc, 1)

        STEPS_A = 5
        PER = 11

        @block.tensor
        def _(pe):
            for turn in range(2):
                pe.wait_ge(link, STEPS_A + turn * (PER - 1) + 3)
                pe.transpose(psA[0:1, 0:P], ends[:, 0:1], k.ident[:])
                pe.transpose(psA[0:1, P:2 * P], ends[:, 1:2], k.ident[:]).then_inc(turned, 1)
                pe.wait_ge(link, STEPS_A + turn * (PER - 1) + 8)
                pe.transpose(psB[:, 0:1], rowsT[0:1, 0, :], k.ident[0:1, 0:1]).then_inc(moved, 1)
            pe.wait_ge(gathered, 16 * BLOCKS)
            for b0 in range(0, BLOCKS, 4):
                for b in range(b0, min(b0 + 4, BLOCKS)):
                    at = (b - b0) * P
                    mm = pe.transpose(psW[:, b0 // 4, at:at + P], wts[:, 0, b, :], k.ident[:])
                mm.then_inc(wT, 1)

        @block.scalar
        def _(act):
            act.wait_ge(link, STEPS_A + 2 * (PER - 1) + 1)
            act.activation(top[:], z[:], ACT.Exp).then_inc(exped, 1)

        @block.gpsimd
        def _(pool):
            pool.wait_ge(out, 32)
            for b in range(BLOCKS):
                pool.indirect_dma_start(wts[:, 0, b, :], None, k.w_d[:],
                                        bass.IndirectOffsetOnAxis(k.chunk_of[:, b:b + 1], 0)).then_inc(gathered, 16)


def stage_messages1(nc, k):
    with ExitStack() as ctx:
        c = Core(nc, ctx)
        SLOTS = 8
        place = c.sb("g_place", [P, 2, SLOTS], I32)
        rows = c.sb("g_rows", [P, SLOTS, D + 1])
        member = c.sb("g_member", [P, SLOTS, P])
        ps = c.ps("g_ps", [P, SLOTS, 512])
        ones, places, gone, members, added, freed = (c.sem("g_" + s) for s in ("ones", "places", "gone", "members", "added", "freed"))
        summed, turns = c.sem("g_summed"), c.sem("g_turns")
        row_in = [c.sem(f"g_row_in{j}") for j in range(SLOTS)]
        block = ctx.enter_context(nc.Block())
        STEPS = ITEMS // SLOTS // 2

        @block.gpsimd
        def _(pool):
            pool.memset(rows[:, :, D:D + 1], 1.0).then_inc(ones, 1)

            def step(i):
                for s in range(2):
                    g = 2 * i + s
                    pool.wait_ge(places, g + 1)
                    for j in range(SLOTS):
                        wait(pool, summed, SLOTS * (g - 1) + j + 1)
                        pool.sem_inc(turns, 1)
                        pool.indirect_dma_start(rows[:, j, 0:D], None, k.h1_d[:],
                                                bass.IndirectOffsetOnAxis(place[:, s, j:j + 1], 0)
                                                ).then_inc(row_in[j], 16)
            repeat(pool, STEPS, step)

        @block.scalar
        def _(act):
            def step(i):
                for s in range(2):
                    g = 2 * i + s
                    wait(act, summed, SLOTS * (g - 1))
                    act.copy(place[:, s], k.place_col[:, bass.ds(g * SLOTS, SLOTS)]).then_inc(places, 1)
            repeat(act, STEPS, step)

        @block.vector
        def _(dve):
            def step(i):
                for s in range(2):
                    g = 2 * i + s
                    for j in range(SLOTS):
                        it = g * SLOTS + j
                        wait(dve, summed, SLOTS * (g - 1) + j + 1)
                        dve.tensor_scalar(member[:, j], k.iota[:], k.cols[:, 4, bass.ds(it, 1)],
                                          k.wcol[:, bass.ds(it, 1)], ALU.is_equal, ALU.mult).then_inc(members, 1)
                    for j in range(SLOTS):
                        it = g * SLOTS + j
                        tile = dve.value_load(k.tile_row[0:1, bass.ds(it, 1)], min_val=0, max_val=TILES - 1)
                        dve.wait_ge(summed, it + 1)
                        wait(dve, added, it)
                        acc = k.acc[:, bass.ds(tile, 1), :].squeeze(1)
                        dve.tensor_tensor(acc, acc, ps[:, j, 0:D + 1], ALU.add).then_inc(added, 1)
            dve.memset(k.acc[:], 0.0).then_inc(freed, 1)
            dve.wait_ge(freed, 1)
            repeat(dve, STEPS, step)

        @block.tensor
        def _(pe):
            pe.wait_ge(ones, 1)

            def step(i):
                for s in range(2):
                    g = 2 * i + s
                    for j in range(SLOTS):
                        it = g * SLOTS + j
                        pe.wait_ge(row_in[j], 16 * (g + 1))
                        pe.wait_ge(members, it + 1)
                        wait(pe, added, it - SLOTS + 1)
                        pe.matmul(ps[:, j, 0:D + 1], member[:, j, :], rows[:, j, :], start=True, stop=True).then_inc(summed, 1)
            repeat(pe, STEPS, step)


def stage_out(nc, k, out):
    with ExitStack() as ctx:
        c = Core(nc, ctx)
        basis = c.sb("o_basis", [P, 2, G, D])
        mean = c.sb("o_mean", [P, G, D])
        den = c.sb("o_den", [P, 2, TILES])
        res = c.sb("o_res", [P, 2, G, D])
        b_in = [c.sem("o_b_in0"), c.sem("o_b_in1")]
        r_out = [c.sem("o_r_out0"), c.sem("o_r_out1")]
        dens, means, sums = (c.sem("o_" + s) for s in ("dens", "means", "sums"))
        block = ctx.enter_context(nc.Block())
        bv = k.basis_d.rearrange("(g t p) d -> g p t d", p=P, t=G)
        ov = out[0:(GROUPS - 1) * G * P, :].rearrange("(g t p) d -> g p t d", p=P, t=G)
        tail = out[(GROUPS - 1) * G * P:, :]
        left = NODES - (GROUPS - 1) * G * P
        m = left // P

        @block.sync
        def _(sp):
            for g in range(GROUPS):
                if g >= 2:
                    sp.wait_ge(sums, g - 1)
                sp.dma_start(basis[:, g % 2], bv[g]).then_inc(b_in[g % 2], 16)

        @block.vector
        def _(dve):
            dve.tensor_scalar(den[:, 0], k.acc[:, :, D], 1e-30, None, ALU.max).then_inc(dens, 1)
            dve.wait_ge(dens, 1)
            dve.reciprocal(den[:, 1], den[:, 0]).then_inc(dens, 1)
            dve.wait_ge(dens, 2)
            for g in range(GROUPS):
                dve.wait_ge(b_in[g % 2], 16 * (g // 2 + 1))
                if g >= 1:
                    dve.wait_ge(sums, g)
                dve.tensor_tensor(mean[:], k.acc[:, g * G:(g + 1) * G, 0:D],
                                  bc(den[:, 1, g * G:(g + 1) * G].unsqueeze(2), [P, G, D]), ALU.mult).then_inc(means, 1)
                dve.wait_ge(means, g + 1)
                if g >= 2:
                    dve.wait_ge(r_out[g % 2], 16 * (g // 2))
                dve.tensor_tensor(res[:, g % 2], mean[:], basis[:, g % 2], ALU.add).then_inc(sums, 1)

        @block.scalar
        def _(act):
            for g in range(GROUPS - 1):
                act.wait_ge(sums, g + 1)
                act.dma_start(ov[g], res[:, g % 2]).then_inc(r_out[g % 2], 16)
            s = (GROUPS - 1) % 2
            act.wait_ge(sums, GROUPS)
            act.dma_start(tail[0:m * P, :].rearrange("(t p) d -> p t d", p=P), res[:, s, 0:m]).then_inc(r_out[s], 16)
            act.dma_start(tail[m * P:left, :], res[0:left - m * P, s, m]).then_inc(r_out[s], 16)
            act.wait_ge(r_out[0], 16 * 7 + (16 if s == 0 else 0))
            act.wait_ge(r_out[1], 16 * 7 + (16 if s == 1 else 0))


class Kept:
    pass


def build(nc, x, src, dst, typ, w, out):
    k = Kept()
    k.src_d = nc.dram_tensor("src_rows", [ROWS, P], F32).ap()
    k.dst_d = nc.dram_tensor("dst_rows", [ROWS, P], F32).ap()
    k.high_d = nc.dram_tensor("high_digits", [3, ROWS, P], BF16).ap()
    k.item_src_d = nc.dram_tensor("item_src", [ITEMS, P], F32).ap()
    k.tile_d = nc.dram_tensor("item_tiles", [ITEMS], I32).ap()
    k.x_d = nc.dram_tensor("x_rows", [NODES_P, D], F32).ap()
    k.pre_d = nc.dram_tensor("pre_rows", [NODES_P, D], F32).ap()
    k.h1_d = nc.dram_tensor("h1_rows", [NODES_P, D], F32).ap()
    k.basis_d = nc.dram_tensor("basis_rows", [NODES_P, D], F32).ap()
    k.z_d = nc.dram_tensor("z_rows", [ROWS, P], F32).ap()
    k.w_d = nc.dram_tensor("w_rows", [ROWS, P], F32).ap()
    k.table_d = [nc.dram_tensor(f"sum_table{t}", [TABLE, D], F32).ap() for t in range(TABLES)]
    with ExitStack() as ctx:
        c = Core(nc, ctx)
        k.ident = c.sb("ident", [P, P])
        k.lower = c.sb("lower", [P, P], BF16)
        k.ones = c.sb("ones", [P, P])
        k.iota = c.sb("iota", [P, P])
        k.iota_p = c.sb("iota_p", [P, 1])
        k.cols = c.sb("cols", [P, 5, ROWS])
        k.tile_row = c.sb("tile_row", [1, ITEMS], I32)
        k.chunk_of = c.sb("chunk_of", [P, BLOCKS], I32)
        k.node_scores = c.sb("node_scores", [P, 2, TILES])
        k.parts = c.sb("table_parts", [P, 3, 3, P], BF16)
        k.split = c.sb("table_split", [P, 3, 2, P])
        k.w1 = c.sb("w1", [P, D + 2])
        k.wg = c.sb("wg", [P, D])
        stage_constants(nc, k)
        stage_edges(nc, k, src, dst, typ)
        with ExitStack() as inner:
            k.u = Core(nc, inner).sb("u", [P, TILES, D])
            stage_nodes0(nc, k, x, w)
            stage_messages0(nc, k)
        stage_weights1(nc, k, w)
        stage_nodes1(nc, k)
        stage_scores(nc, k)
        k.wcol = c.sb("w_cols", [P, ITEMS])
        k.place_col = c.sb("place_cols", [P, ITEMS], I32)
        stage_softmax(nc, k)
        stage_places(nc, k)
        k.acc = c.sb("acc", [P, TILES, D + 1])
        stage_messages1(nc, k)
        stage_out(nc, k, out)
    return nc


def stage_places(nc, k):
    with ExitStack() as ctx:
        block = ctx.enter_context(nc.Block())

        @block.vector
        def _(dve):
            dve.tensor_scalar(k.place_col[:], k.cols[:, 3], float(PAD_NODE), None, ALU.min)


_EDGE = ("src", "dst", "edge_type_460")


def kernel(**inputs):
    import numpy as _np
    import concourse.bacc as _bacc
    from concourse import mybir as _mybir
    from concourse.bass_utils import run_bass_kernel_spmd as _run

    nc = _bacc.Bacc("TRN2", target_bir_lowering=False, num_devices=1)
    arrays, args = {}, {}
    for name in inputs:
        a = _np.ascontiguousarray(inputs[name])
        arrays[f"in_{name}"] = a
        args[name] = nc.dram_tensor(f"in_{name}", a.shape, _mybir.dt.from_np(a.dtype), kind="ExternalInput").ap()
    out = nc.dram_tensor("out_rows", [NODES, D], F32, kind="ExternalOutput").ap()
    build(nc, args["x"], *(args[n] for n in _EDGE), args, out)
    r = _run(nc, [arrays], core_ids=[0])
    return r.results[0]["out_rows"]
```

```python
from contextlib import ExitStack

import concourse.bass as bass
from concourse import mybir

F32 = mybir.dt.float32
BF16 = mybir.dt.bfloat16
I32 = mybir.dt.int32
ALU = mybir.AluOpType
ACT = mybir.ActivationFunctionType
AX = mybir.AxisListType.X

P = 128
NODES, D = 12500, 128
EDGES = 200000
RELS = 460
TILES = -(-NODES // P)
NODES_P = TILES * P
PAD_NODE = NODES_P - 1
CHUNKS = -(-EDGES // P)
BLOCKS = -(-(CHUNKS + TILES) // P)
ROWS = BLOCKS * P
ITEMS = ROWS
TABLE = NODES_P + P
TABLES = 4
G = 7
GROUPS = TILES // G
EPS = 1e-5
SLOPE = 0.01
LOW = -1e30
RELTILES = -(-RELS // P)
STACK = 3 * RELTILES
ZG = 64
ZDST = ROWS // ZG
ZSRC = 18
ZP = 16
ZP_GROUPS = -(-(CHUNKS - ZG * ZSRC) // ZP // 2) * 2
SCAN = CHUNKS


def wait(eng, sem, value):
    if isinstance(value, int) and value <= 0:
        return
    eng.wait_ge(sem, value)


def repeat(eng, count, step):
    step(0)
    with eng.Fori(1, count) as i:
        step(i)


class Core:

    def __init__(self, nc, ctx, clears=False):
        self.nc, self.ctx = nc, ctx
        self.cleared = [] if clears else None
        if clears:
            ctx.callback(nc.all_engine_barrier)
            ctx.callback(nc.clear_and_free_semaphores, self.cleared)

    def sb(self, name, shape, dt=F32):
        return self.ctx.enter_context(self.nc.sbuf_tensor(name, shape, dt))

    def ps(self, name, shape, dt=F32):
        return self.ctx.enter_context(self.nc.psum_tensor(name, shape, dt))

    def sem(self, name):
        if self.cleared is not None:
            self.cleared.append(self.nc.alloc_semaphore(name=name))
            return self.cleared[-1]
        return self.ctx.enter_context(self.nc.semaphore(name))


def group(ap, g):
    return ap[g] if isinstance(g, int) else ap[bass.ds(g, 1)].squeeze(0)


def load_numbers(nc, engine, ap, top):
    return nc.values_load_multi_w_load_instructions(ap, engines=(engine,), min_val=0, max_val=top)[1]


def bc(ap, shape):
    return ap.to_broadcast(shape)


def stage_constants(nc, k):
    with ExitStack() as ctx:
        c = Core(nc, ctx)
        zeroed, made = c.sem("c_zeroed"), c.sem("c_made")
        ramp = c.sb("c_ramp", [P, P], I32)
        part = c.sb("c_part", [P, 1], I32)
        block = ctx.enter_context(nc.Block())

        @block.gpsimd
        def _(pool):
            pool.memset(k.ident[:], 0.0).then_inc(zeroed, 1)
            pool.memset(k.upper[:], 1.0).then_inc(zeroed, 1)
            pool.iota(ramp[:], [[1, P]], base=0, channel_multiplier=0).then_inc(zeroed, 1)
            pool.iota(part[:], [[1, 1]], base=0, channel_multiplier=1).then_inc(zeroed, 1)
            pool.wait_ge(zeroed, 4)
            pool.affine_select(out=k.ident[:], in_=k.ident[:], compare_op=ALU.not_equal, fill=1.0,
                               base=0, pattern=[[-1, P]], channel_multiplier=1).then_inc(made, 1)
            pool.affine_select(out=k.upper[:], in_=k.upper[:], compare_op=ALU.is_gt, fill=0.0,
                               base=0, pattern=[[1, P]], channel_multiplier=-1).then_inc(made, 1)

        @block.vector
        def _(dve):
            dve.memset(k.ones[:], 1.0)
            dve.memset(k.onesb[:], 1.0)
            dve.wait_ge(zeroed, 4)
            dve.tensor_copy(k.iota[:], ramp[:])
            dve.tensor_copy(k.iota_p[:], part[:])
            dve.wait_ge(made, 2)


def stage_load(nc, k, src, dst, typ):
    with ExitStack() as ctx:
        c = Core(nc, ctx)
        runs, run = EDGES // 1600, 1600
        assert runs * run == EDGES and runs <= P
        flat = c.sb("l_flat", [runs, run], I32)
        follower = c.sb("l_follower", [P, 1], I32)
        falls = c.sb("l_falls", [P, run])
        fell = c.sb("l_fell", [P, 1])
        total = c.ps("l_total", [P, 512])
        ready, loaded, flat_in, fallen, counted = (
            c.sem("l_" + s) for s in ("ready", "loaded", "flat_in", "fallen", "counted"))
        block = ctx.enter_context(nc.Block())
        full = EDGES // (P * P)
        whole = EDGES // P - full * P
        rest = EDGES % P

        @block.sync
        def _(sp):
            sp.dma_start(flat[:], dst.rearrange("(p j) -> p j", j=run)).then_inc(flat_in, 16)
            sp.wait_ge(ready, 4)
            with nc.allow_non_contiguous_dma("124 single numbers"):
                sp.dma_start(follower[0:runs - 1, :], dst.rearrange("(p j) -> p j", j=run)[1:runs, 0:1]).then_inc(flat_in, 16)
            for n, a in enumerate((src, dst, typ)):
                at = full * P * P
                sp.dma_start(k.raw[:, n, 0:full, :],
                             a[0:at].rearrange("(b p f) -> p b f", p=P, f=P)).then_inc(loaded, 16)
                sp.dma_start(k.raw[0:whole, n, full, :],
                             a[at:at + whole * P].rearrange("(p f) -> p f", f=P)).then_inc(loaded, 16)
                sp.dma_start(k.raw[whole:whole + 1, n, full, 0:rest],
                             a[at + whole * P:EDGES].rearrange("(p f) -> p f", p=1)).then_inc(loaded, 16)
            sp.wait_ge(loaded, 16 * 9)

        @block.vector
        def _(dve):
            for n, pad in enumerate((PAD_NODE, PAD_NODE, 0)):
                dve.memset(k.raw[:, n, full, :], pad).then_inc(ready, 1)
            dve.memset(follower[:], NODES_P).then_inc(ready, 1)
            dve.memset(falls[:], 0.0).then_inc(fallen, 1)
            dve.wait_ge(fallen, 1)
            dve.wait_ge(flat_in, 32)
            dve.tensor_tensor(falls[0:runs, 0:run - 1], flat[:, 0:run - 1], flat[:, 1:run], ALU.is_gt).then_inc(fallen, 1)
            dve.tensor_tensor(falls[0:runs, run - 1:run], flat[:, run - 1:run], follower[0:runs], ALU.is_gt).then_inc(fallen, 1)
            dve.wait_ge(fallen, 3)
            dve.tensor_reduce(fell[:], falls[:], AX, ALU.add).then_inc(fallen, 1)
            dve.wait_ge(counted, 1)
            dve.tensor_scalar(k.unsorted[:], total[0:1, 0:1], 1.0, None, ALU.min)

        @block.tensor
        def _(pe):
            pe.wait_ge(fallen, 4)
            pe.matmul(total[:, 0:1], k.ones[:], fell[:], start=True, stop=True).then_inc(counted, 1)


def stage_sort(nc, k):
    with ExitStack() as ctx:
        c = Core(nc, ctx)
        rowsf = c.sb("r_rows", [P, 3, BLOCKS, P])
        record = c.sb("r_record", [P, ROWS, 4], I32)
        digit_i = c.sb("r_digit_i", [P, ROWS], I32)
        digit = c.sb("r_digit", [P, ROWS])
        hot = c.sb("r_hot", [P, P], BF16)
        onesb = c.sb("r_onesb", [P, P], BF16)
        start = c.sb("r_start", [P, P])
        scan = c.sb("r_scan", [P, P])
        spot = c.sb("r_spot", [P, P])
        rank = c.sb("r_rank", [P, 1])
        place = c.sb("r_place", [P, 1], I32)
        sent = c.sb("r_sent", [P, 4], I32)
        again = c.sb("r_again", [P, BLOCKS, P * 4], I32)
        psT = c.ps("r_psT", [P, 2, 512])
        psC = c.ps("r_psC", [P, 512])
        psR = c.ps("r_psR", [P, 512])
        d = nc.dram_tensor("sorted_records", [ROWS * P, 4], I32).ap()
        SEND_LINKS = 4
        for turn in range(2):
            with ExitStack() as inner:
                q = Core(nc, inner, clears=True)
                (rows_made, turned, taken, digits, hots, counted, link, ranked, placed, landed, loaded, read,
                 turns) = (q.sem(f"r{turn}_" + s) for s in (
                     "rows_made", "turned", "taken", "digits", "hots", "counted", "link", "ranked", "placed", "landed",
                     "loaded", "read", "turns"))
                block = inner.enter_context(nc.Block())

                @block.vector
                def _(dve):
                    dve.tensor_copy(rowsf[:], k.raw[:]).then_inc(rows_made, 1)
                    dve.memset(record[:, :, 3], 0).then_inc(rows_made, 1)
                    dve.memset(onesb[:], 1.0).then_inc(rows_made, 1)
                    dve.memset(start[:], 0.0).then_inc(rows_made, 1)
                    dve.wait_ge(taken, 3 * BLOCKS)
                    dve.tensor_scalar(digit_i[:], record[:, :, 1], 7 if turn else P - 1, None,
                                      ALU.arith_shift_right if turn else ALU.bitwise_and).then_inc(digits, 1)
                    dve.wait_ge(digits, 1)
                    dve.tensor_copy(digit[:], digit_i[:]).then_inc(digits, 1)
                    dve.wait_ge(digits, 2)
                    dve.wait_ge(rows_made, 4)

                    def count(i):
                        wait(dve, counted, i)
                        dve.tensor_scalar(hot[:], k.iota[:], digit[:, bass.ds(i, 1)], None, ALU.is_equal).then_inc(hots, 1)
                        dve.wait_ge(counted, i + 1)
                        wait(dve, link, i)
                        dve.tensor_tensor(start[:], start[:], psC[:, 0:P], ALU.add).then_inc(link, 1)
                    repeat(dve, ROWS, count)
                    dve.wait_ge(link, ROWS)
                    dve.tensor_tensor_scan(scan[:], start[:], start[:], 0.0, ALU.add, ALU.bypass).then_inc(link, 1)
                    dve.wait_ge(link, ROWS + 1)
                    dve.tensor_tensor(start[:], scan[:], start[:], ALU.subtract).then_inc(link, 1)
                    dve.wait_ge(link, ROWS + 2)

                    def send(i):
                        base = ROWS + 2 + SEND_LINKS * i
                        wait(dve, ranked, i)
                        dve.tensor_scalar(hot[:], k.iota[:], digit[:, bass.ds(i, 1)], None, ALU.is_equal).then_inc(hots, 1)
                        dve.wait_ge(ranked, i + 1)
                        dve.tensor_tensor(spot[:], start[:], psR[:, 0:P], ALU.add).then_inc(link, 1)
                        dve.wait_ge(link, base + 1)
                        dve.scalar_tensor_tensor(scan[:], k.iota[:], digit[:, bass.ds(i, 1)], spot[:],
                                                 ALU.is_equal, ALU.mult, accum_out=rank[:]).then_inc(link, 1)
                        dve.tensor_tensor(start[:], start[:], psC[:, 0:P], ALU.add).then_inc(link, 1)
                        wait(dve, read, i)
                        dve.tensor_copy(sent[:], record[:, bass.ds(i, 1), :].squeeze(1)).then_inc(link, 1)
                        dve.wait_ge(link, base + 4)
                        dve.tensor_copy(place[:], rank[:]).then_inc(placed, 1)
                    repeat(dve, ROWS, send)
                    for n in range(3):
                        dve.wait_ge(loaded, 16)
                        dve.tensor_copy(k.raw[:, n], again[:].rearrange("p b (f w) -> p b f w", w=4)[:, :, :, n])

                @block.tensor
                def _(pe):
                    pe.wait_ge(rows_made, 1)
                    for m in range(3 * BLOCKS):
                        n, b = divmod(m, BLOCKS)
                        if m >= 2:
                            pe.wait_ge(taken, m - 1)
                        pe.transpose(psT[:, m % 2, 0:P], rowsf[:, n, b, :], k.ident[:]).then_inc(turned, 1)
                    pe.wait_ge(rows_made, 3)

                    def count(i):
                        pe.wait_ge(hots, i + 1)
                        wait(pe, link, i)
                        pe.matmul(psC[:, 0:P], onesb[:], hot[:], start=True, stop=True).then_inc(counted, 1)
                    repeat(pe, ROWS, count)

                    def send(i):
                        pe.wait_ge(hots, ROWS + i + 1)
                        pe.wait_ge(link, ROWS + 2 + SEND_LINKS * i)
                        pe.matmul(psC[:, 0:P], onesb[:], hot[:], start=True, stop=True)
                        pe.matmul(psR[:, 0:P], k.upper[:], hot[:], start=True, stop=True).then_inc(ranked, 1)
                    repeat(pe, ROWS, send)

                @block.scalar
                def _(act):
                    for m in range(3 * BLOCKS):
                        n, b = divmod(m, BLOCKS)
                        act.wait_ge(turned, m + 1)
                        act.copy(record[:, b * P:(b + 1) * P, n], psT[:, m % 2, 0:P]).then_inc(taken, 1)

                @block.gpsimd
                def _(pool):
                    def send(i):
                        pool.wait_ge(placed, i + 1)
                        pool.sem_inc(turns, 1)
                        pool.indirect_dma_start(d, bass.IndirectOffsetOnAxis(place[:, 0:1], 0), sent[:], None
                                                ).then_inc(landed, 16)
                        pool.wait_ge(landed, 16 * (i + 1))
                        pool.sem_inc(read, 1)
                    repeat(pool, ROWS, send)

                @block.sync
                def _(sp):
                    sp.wait_ge(read, ROWS)
                    sp.dma_start(again[:], d.rearrange("(b p f) w -> p b (f w)", p=P, f=P)).then_inc(loaded, 16)
                    sp.wait_ge(loaded, 16)


def stage_edges(nc, k):
    with ExitStack() as ctx:
        c = Core(nc, ctx, clears=True)
        raw = k.raw
        high = c.sb("e_high", [P, 3, BLOCKS, P], I32)
        highb = c.sb("e_highb", [P, 3, BLOCKS, P], BF16)
        rows = c.sb("e_rows", [P, 2, BLOCKS, P])
        turn = c.sb("e_turn", [P, 5, BLOCKS, P])
        item = c.sb("e_item", [P, 2, BLOCKS, P])
        mask = c.sb("e_mask", [P, BLOCKS, P])
        spare = c.sb("e_spare", [P, P])
        first_tile = c.sb("e_first", [P, BLOCKS])
        below = c.sb("e_below", [P, TILES, BLOCKS])
        below2 = c.sb("e_below2", [P, BLOCKS, TILES])
        count = c.sb("e_count", [P, TILES])
        last = c.sb("e_last", [P, TILES])
        item_no_i = c.sb("e_item_no_i", [P, BLOCKS], I32)
        item_no = c.sb("e_item_no", [P, BLOCKS])
        tile_of = c.sb("e_tile", [P, BLOCKS])
        tile_node = c.sb("e_tile_node", [P, BLOCKS])
        tile_rows = c.sb("e_tile_rows", [BLOCKS, P], I32)
        totals = c.ps("e_totals", [P, 512])
        turned = c.ps("e_turned", [P, 6, 4, P])
        made, stored = c.sem("e_made"), c.sem("e_stored")
        counted, walked, gathered, masked = c.sem("e_counted"), c.sem("e_walked"), c.sem("e_gathered"), c.sem("e_masked")
        done, copied, kept, numbered = c.sem("e_done"), c.sem("e_copied"), c.sem("e_kept"), c.sem("e_numbered")
        tiles_out, tiles_in, digits_out = c.sem("e_tiles_out"), c.sem("e_tiles_in"), c.sem("e_digits_out")
        block = ctx.enter_context(nc.Block())
        @block.sync
        def _(sp):
            sp.wait_ge(made, 1)
            for n, d in enumerate((k.src_d, k.dst_d)):
                sp.dma_start(d.rearrange("(b p) f -> p b f", p=P), rows[:, n]).then_inc(stored, 16)
            sp.wait_ge(made, 4)
            for n in range(3):
                sp.dma_start(k.high_d[n].rearrange("(b p) f -> p b f", p=P), highb[:, n]).then_inc(digits_out, 16)
            sp.wait_ge(masked, 5)
            sp.dma_start(k.item_src_d.rearrange("(b p) f -> p b f", p=P), turn[:, 3]).then_inc(kept, 16)
            sp.wait_ge(masked, 6)
            sp.dma_start(k.item_dst_d.rearrange("(b p) f -> p b f", p=P), highb[:, 0]).then_inc(kept, 16)
            sp.wait_ge(copied, 1)
            sp.dma_start(k.tile_d.rearrange("(b p) -> b p", p=P), tile_rows[:]).then_inc(tiles_out, 16)
            sp.wait_ge(tiles_out, 16)
            sp.dma_start(k.tile_row[:], k.tile_d.rearrange("(a p) -> a p", a=1)).then_inc(tiles_in, 16)
            sp.wait_ge(tiles_in, 16)
            sp.wait_ge(kept, 32)

        @block.gpsimd
        def _(pool):
            pool.iota(item_no_i[:], [[P, BLOCKS]], base=0, channel_multiplier=1).then_inc(numbered, 1)
            pool.wait_ge(stored, 32)
            pool.wait_ge(walked, 5)
            for b in range(BLOCKS):
                for n, d in enumerate((k.src_d, k.dst_d)):
                    pool.indirect_dma_start(item[:, n, b, :], None, d[:],
                                            bass.IndirectOffsetOnAxis(k.chunk_of[:, b:b + 1], 0)
                                            ).then_inc(gathered, 16)

        @block.vector
        def _(dve):
            dve.tensor_scalar(spare[:], k.iota[:], float(NODES_P), None, ALU.add)
            dve.tensor_copy(rows[:], raw[:, 0:2]).then_inc(made, 1)
            dve.tensor_scalar(high[:], raw[:], 7, None, ALU.arith_shift_right).then_inc(made, 1)
            dve.wait_ge(made, 2)
            dve.tensor_scalar(raw[:], raw[:], P - 1, None, ALU.bitwise_and).then_inc(made, 1)
            dve.tensor_copy(highb[:], high[:]).then_inc(made, 1)
            dve.wait_ge(made, 3)
            dve.tensor_copy(turn[:, 0:3:2], raw[:, 0:3:2])
            dve.tensor_copy(turn[:, 1], rows[:, 0]).then_inc(made, 1)
            dve.tensor_copy(first_tile[:], high[:, 1, :, 0]).then_inc(made, 1)
            dve.wait_ge(made, 6)
            dve.tensor_tensor(below[:], bc(first_tile[:].unsqueeze(1), [P, TILES, BLOCKS]),
                              bc(k.iota[:, 0:TILES].unsqueeze(2), [P, TILES, BLOCKS]), ALU.is_le).then_inc(made, 1)
            dve.wait_ge(made, 7)
            dve.tensor_reduce(count[:], below[:], AX, ALU.add).then_inc(made, 1)
            dve.wait_ge(counted, 1)
            dve.tensor_scalar(last[:], totals[:, 0:TILES], 1.0, float(CHUNKS), ALU.max, ALU.min).then_inc(walked, 1)
            dve.wait_ge(numbered, 1)
            dve.tensor_copy(item_no[:], item_no_i[:]).then_inc(walked, 1)
            dve.wait_ge(walked, 2)
            dve.tensor_tensor(last[:], last[:], k.iota[:, 0:TILES], ALU.add).then_inc(made, 1)
            dve.wait_ge(made, 9)
            dve.tensor_tensor(below2[:], bc(last[:].unsqueeze(1), [P, BLOCKS, TILES]),
                              bc(item_no[:].unsqueeze(2), [P, BLOCKS, TILES]), ALU.is_le).then_inc(made, 1)
            dve.wait_ge(made, 10)
            dve.tensor_reduce(tile_of[:], below2[:], AX, ALU.add).then_inc(made, 1)
            dve.wait_ge(made, 11)
            dve.tensor_scalar(tile_of[:], tile_of[:], float(TILES - 1), None, ALU.min).then_inc(walked, 1)
            dve.wait_ge(walked, 3)
            dve.tensor_scalar(tile_node[:], tile_of[:], float(P), None, ALU.mult).then_inc(walked, 1)
            dve.tensor_tensor(k.chunk_of[:], item_no[:], tile_of[:], ALU.subtract).then_inc(walked, 1)
            dve.wait_ge(walked, 5)
            dve.wait_ge(gathered, 16 * 2 * BLOCKS)
            dve.tensor_tensor(turn[:, 4], item[:, 1], bc(tile_node[:].unsqueeze(2), [P, BLOCKS, P]),
                              ALU.subtract).then_inc(masked, 1)
            dve.wait_ge(masked, 1)
            dve.tensor_scalar(mask[:], turn[:, 4], 0.0, None, ALU.is_ge).then_inc(masked, 1)
            dve.wait_ge(masked, 2)
            dve.scalar_tensor_tensor(mask[:], turn[:, 4], float(P), mask[:], ALU.is_lt, ALU.mult).then_inc(masked, 1)
            wide = bc(spare[:].unsqueeze(1), [P, BLOCKS, P])
            dve.tensor_tensor(item[:, 0], item[:, 0], wide, ALU.subtract).then_inc(made, 1)
            dve.wait_ge(masked, 3)
            dve.wait_ge(made, 12)
            dve.tensor_tensor(item[:, 0], item[:, 0], mask[:], ALU.mult).then_inc(masked, 1)
            dve.wait_ge(masked, 4)
            dve.tensor_tensor(turn[:, 3], item[:, 0], wide, ALU.add).then_inc(masked, 1)
            dve.wait_ge(digits_out, 48)
            dve.tensor_copy(highb[:, 0], turn[:, 4]).then_inc(masked, 1)
            dve.wait_ge(done, 16)
            dve.tensor_scalar(k.place_col[:], k.cols[:, 3], float(PAD_NODE), None, ALU.min)

        quads = [(n, b) for n in range(5) for b in range(0, BLOCKS, 4)]

        @block.tensor
        def _(pe):
            pe.wait_ge(made, 8)
            pe.matmul(totals[:, 0:TILES], k.ones[:], count[:], start=True, stop=True).then_inc(counted, 1)
            pe.wait_ge(walked, 3)
            pe.transpose(totals[0:BLOCKS, P:2 * P], tile_of[:], k.ident[:]).then_inc(counted, 1)
            for q, (n, b0) in enumerate(quads):
                if n == 3:
                    pe.wait_ge(masked, 5)
                if q >= 6:
                    pe.wait_ge(done, q - 5)
                for b in range(b0, min(b0 + 4, BLOCKS)):
                    mm = pe.transpose(turned[:, q % 6, b - b0, :], turn[:, n, b, :], k.ident[:])
                mm.then_inc(counted, 1)

        @block.scalar
        def _(act):
            act.wait_ge(counted, 2)
            act.copy(tile_rows[:], totals[0:BLOCKS, P:2 * P]).then_inc(copied, 1)
            for q, (n, b0) in enumerate(quads):
                act.wait_ge(counted, q + 3)
                m = min(4, BLOCKS - b0)
                act.copy(k.cols[:, n, b0 * P:(b0 + m) * P], turned[:, q % 6, 0:m, :]).then_inc(done, 1)


def stage_nodes0(nc, k, x, w):
    with ExitStack() as ctx:
        c = Core(nc, ctx)
        weights = c.sb("n_weights", [P, 2, D])
        biases = c.sb("n_biases", [P, 3, D])
        sq = c.sb("n_sq", [P, 2, G, D])
        h = c.sb("n_h", [P, 2, G, D])
        hT = c.sb("n_hT", [P, 2, G, P])
        gate_in = c.sb("n_gate_in", [P, 2, G, D])
        pre = c.sb("n_pre", [P, 2, G, D])
        sums = c.sb("n_sums", [P, 3, TILES])
        psT = c.ps("n_psT", [P, 2, 8, P])
        psM = c.ps("n_psM", [P, 8, 2, D])
        zero = c.sb("n_zero", [P, D])
        held, noted, copied, wts, zeroed, tables, tail_in, bias_in, biased = (
            c.sem("n_" + s) for s in ("held", "noted", "copied", "wts", "zeroed", "tables", "tail_in", "bias_in", "biased"))
        out = [c.sem("n_out0"), c.sem("n_out1")]
        x_in = [c.sem("n_x_in0"), c.sem("n_x_in1")]
        link, centred, squared, varied, rooted, scaled, summed = (
            c.sem("n_" + s) for s in ("link", "centred", "squared", "varied", "rooted", "scaled", "summed"))
        hs, turned, copies, mult, sigs, pres, us = (
            c.sem("n_" + s) for s in ("hs", "turned", "copies", "mult", "sigs", "pres", "us"))
        block = ctx.enter_context(nc.Block())
        prev = k.pre_d.rearrange("(g t p) d -> g p t d", p=P, t=G)

        def rows_of(g):
            return k.u[:, bass.ds(g * G, G), :]

        def of(n, g):
            return sums[:, n, bass.ds(g * G, G)]

        @block.sync
        def _(sp):
            xv = x[0:(GROUPS - 1) * G * P, :].rearrange("(g t p) d -> g p t d", p=P, t=G)

            def step(i):
                for s in range(2):
                    g = 2 * i + s
                    wait(sp, x_in[s], 16 * i)
                    sp.dma_start(rows_of(g), group(xv, g)).then_inc(x_in[s], 16)
            repeat(sp, GROUPS // 2 - 1, step)
            g = GROUPS - 2
            sp.dma_start(rows_of(g), xv[g]).then_inc(x_in[0], 16)
            sp.wait_ge(zeroed, 2)
            at = (GROUPS - 1) * G * P
            whole = (NODES - at) // P
            sp.dma_start(k.u[:, (GROUPS - 1) * G:(GROUPS - 1) * G + whole, :],
                         x[at:at + whole * P, :].rearrange("(t p) d -> p t d", p=P)).then_inc(x_in[1], 16)
            sp.dma_start(k.u[0:NODES - at - whole * P, TILES - 1, :], x[at + whole * P:NODES, :]).then_inc(tail_in, 16)
            for n, name in enumerate(("L0_gnn_Wa_w", "L0_gnn_Wn_w")):
                sp.dma_start(weights[:, n, :], w[name]).then_inc(wts, 16)
            for n, name in enumerate(("L0_gnn_Wa_b", "L0_gnn_Wn_b", "L0_gnn_Wg_b")):
                sp.dma_start(biases[:, n, :], w[name].partition_broadcast(P)).then_inc(bias_in, 16)
            sp.dma_start(k.x_d[0:NODES, :], x).then_inc(copied, 16)
            sp.dma_start(k.x_d[NODES:NODES_P, :], zero[0:NODES_P - NODES, :]).then_inc(copied, 16)
            sp.wait_ge(copied, 32)

        @block.gpsimd
        def _(pool):
            pool.memset(zero[:], 0.0).then_inc(zeroed, 1)
            pool.memset(k.u[:, TILES - 1, :], 0.0).then_inc(zeroed, 1)

            def hold(i):
                for s in range(2):
                    g = 2 * i + s
                    pool.wait_ge(hs, g + 1)
                    pool.tensor_copy(rows_of(g), h[:, s]).then_inc(held, 1)
            repeat(pool, GROUPS // 2, hold)

        @block.vector
        def _(dve):
            dve.wait_ge(bias_in, 48)
            dve.tensor_tensor(biases[:, 1], biases[:, 1], biases[:, 2], ALU.add).then_inc(biased, 1)

            def centre(i):
                for s in range(2):
                    g = 2 * i + s
                    dve.wait_ge(x_in[s], 16 * (i + 1))
                    dve.tensor_reduce(of(0, g), rows_of(g), AX, ALU.add).then_inc(link, 1)
                    dve.wait_ge(link, 2 * g + 1)
                    dve.tensor_scalar(of(1, g), of(0, g), -1.0 / D, None, ALU.mult).then_inc(link, 1)
                    dve.wait_ge(link, 2 * g + 2)
                    dve.tensor_tensor(rows_of(g), rows_of(g), bc(of(1, g).unsqueeze(2), [P, G, D]), ALU.add).then_inc(centred, 1)
                    if not (isinstance(g, int) and g == 0):
                        spread(g - 1, 1 - s)

            def spread(g, s):
                dve.wait_ge(squared, g + 1)
                dve.sem_inc(noted, 1)
                dve.tensor_reduce(of(0, g), sq[:, s], AX, ALU.add).then_inc(varied, 1)

            repeat(dve, GROUPS // 2 - 1, centre)
            dve.wait_ge(tail_in, 16)
            centre(GROUPS // 2 - 1)
            spread(GROUPS - 1, 1)
            dve.wait_ge(varied, GROUPS)
            dve.tensor_scalar(sums[:, 1], sums[:, 0], 1.0 / D, EPS, ALU.mult, ALU.add).then_inc(varied, 1)
            dve.wait_ge(rooted, 1)
            dve.reciprocal(sums[:, 0], sums[:, 2]).then_inc(scaled, 1)
            dve.wait_ge(scaled, 1)

            def scale(g, s):
                wait(dve, turned, g - 1)
                wait(dve, held, g - 1)
                dve.scalar_tensor_tensor(h[:, s], rows_of(g), 0.0, bc(of(0, g).unsqueeze(2), [P, G, D]),
                                         ALU.max, ALU.mult).then_inc(hs, 1)

            def step(i):
                for s in range(2):
                    g = 2 * i + s
                    if not (isinstance(g, int) and g == GROUPS - 1):
                        scale(g + 1, 1 - s)
                    if not (isinstance(g, int) and g == 0):
                        add_biases(g - 1, 1 - s, i if s else i - 1)
                    if not (isinstance(g, int) and g < 2):
                        gated(g - 2, s)

            def add_biases(g, s, i):
                dve.wait_ge(mult, g + 1)
                wait(dve, us, g - 1)
                dve.tensor_tensor(gate_in[:, s], psM[:, 0:G, 0, :], bc(biases[:, 0].unsqueeze(1), [P, G, D]), ALU.add).then_inc(summed, 1)
                wait(dve, out[s], 16 * i)
                dve.tensor_tensor(pre[:, s], psM[:, 0:G, 1, :], bc(biases[:, 1].unsqueeze(1), [P, G, D]), ALU.add).then_inc(pres, 1)

            def gated(g, s):
                dve.wait_ge(sigs, g + 1)
                dve.wait_ge(held, g + 1)
                dve.tensor_tensor(rows_of(g), rows_of(g), gate_in[:, s], ALU.mult).then_inc(us, 1)

            dve.wait_ge(biased, 1)
            scale(0, 0)
            repeat(dve, GROUPS // 2 - 1, step)
            step(GROUPS // 2 - 1)
            add_biases(GROUPS - 1, 1, GROUPS // 2 - 1)
            gated(GROUPS - 2, 0)
            gated(GROUPS - 1, 1)

        @block.tensor
        def _(pe):
            pe.wait_ge(wts, 32)

            def turn(g, s):
                pe.wait_ge(hs, g + 1)
                wait(pe, copies, g - 1)
                for t in range(G):
                    mm = pe.transpose(psT[:, s, t, :], h[:, s, t, :], k.ident[:])
                mm.then_inc(turned, 1)

            def product(g, s):
                pe.wait_ge(copies, g + 1)
                wait(pe, pres, g)
                for t in range(G):
                    mm = pe.matmul(psM[:, t], hT[:, s, t, :], weights[:], start=True, stop=True)
                mm.then_inc(mult, 1)

            def step(i):
                for s in range(2):
                    g = 2 * i + s
                    turn(g, s)
                    if not (isinstance(g, int) and g == 0):
                        product(g - 1, 1 - s)
            repeat(pe, GROUPS // 2, step)
            product(GROUPS - 1, 1)

        @block.scalar
        def _(act):
            act.wait_ge(zeroed, 1)

            def empty(t):
                act.dma_start(k.table_d[t].rearrange("(t p) d -> p t d", p=P),
                              bc(zero[:].unsqueeze(1), [P, TABLE // P, D])).then_inc(tables, 16)
            for t in range(TABLES // 2):
                empty(t)

            def square(i):
                for s in range(2):
                    g = 2 * i + s
                    act.wait_ge(centred, g + 1)
                    wait(act, varied, g - 1)
                    act.activation(sq[:, s], rows_of(g), ACT.Square).then_inc(squared, 1)
            repeat(act, GROUPS // 2, square)
            act.wait_ge(varied, GROUPS + 1)
            act.activation(sums[:, 2], sums[:, 1], ACT.Sqrt).then_inc(rooted, 1)
            for t in range(TABLES // 2, TABLES):
                empty(t)

            def copy(g, s):
                act.wait_ge(turned, g + 1)
                wait(act, mult, g - 1)
                act.copy(hT[:, s], psT[:, s, 0:G]).then_inc(copies, 1)

            def gate(g, s):
                act.wait_ge(summed, g + 1)
                act.activation(gate_in[:, s], gate_in[:, s], ACT.Sigmoid).then_inc(sigs, 1)
                act.wait_ge(pres, g + 1)
                act.dma_start(group(prev, g), pre[:, s]).then_inc(out[s], 16)

            def step(i):
                copy(2 * i, 0)
                if not isinstance(i, int):
                    gate(2 * i - 1, 1)
                copy(2 * i + 1, 1)
                gate(2 * i, 0)

            repeat(act, GROUPS // 2, step)
            gate(GROUPS - 1, 1)
            act.wait_ge(tables, 16 * TABLES)
            for s in range(2):
                act.wait_ge(out[s], 16 * (GROUPS // 2))


def stage_messages0(nc, k):
    with ExitStack() as ctx:
        c = Core(nc, ctx)
        RING = 4
        wide = c.sb("m_wide", [P, 2, TABLES, P])
        same = c.sb("m_same", [P, 2, TABLES, P], BF16)
        member = c.sb("m_member", [P, 2, TABLES, P], BF16)
        later = c.sb("m_later", [P, 2, TABLES, P], BF16)
        spare = c.sb("m_spare", [P, 1])
        first = c.sb("m_first", [P, 2, TABLES])
        place = c.sb("m_place", [P, RING, TABLES], I32)
        mix = c.sb("m_mix", [P, 2, TABLES, P])
        rows = c.sb("m_rows", [P, RING, TABLES, D])
        high = c.sb("m_high", [STACK, 2, TABLES * P], BF16)
        pick = c.sb("m_pick", [STACK, 2, TABLES * P], BF16)
        junk = c.sb("m_junk", [P, 2, TABLES, P])
        ps_mix = c.ps("m_ps_mix", [P, 2, TABLES, P])
        ps_rows = c.ps("m_ps_rows", [P, 2, TABLES, D])
        ps_type = c.ps("m_ps_type", [P, 2, TABLES, P])
        ps_count = c.ps("m_ps_count", [P, 2, 512])
        wide_in = [c.sem("m_wide_in0"), c.sem("m_wide_in1")]
        spared, sames, members, laters, picks, counts, firsts, places, types = (
            c.sem("m_" + s) for s in ("spared", "sames", "members", "laters", "picks", "counts", "firsts", "places", "types"))
        mixed, mixes, looked, summed, rowed = (c.sem("m_" + s) for s in ("mixed", "mixes", "looked", "summed", "rowed"))
        added = [c.sem(f"m_added{t}") for t in range(TABLES)]
        sent, turns = c.sem("m_sent"), c.sem("m_turns")
        block = ctx.enter_context(nc.Block())
        LAST = ITEMS // TABLES - 1
        STEPS = ITEMS // TABLES // RING
        assert STEPS * TABLES * RING == ITEMS
        srcs = k.item_src_d.rearrange("(g t) e -> g (t e)", t=TABLES)
        highs = k.high_d[2].rearrange("(g t) e -> g (t e)", t=TABLES)

        @block.sync
        def _(sp):
            def step(i):
                for r in range(RING):
                    g, s = RING * i + r, r % 2
                    wait(sp, sames, g - 1)
                    wait(sp, picks, g - 1)
                    sp.dma_start(wide[:, s].rearrange("p t e -> p (t e)"),
                                 group(srcs, g).partition_broadcast(P)).then_inc(wide_in[s], 16)
                    sp.dma_start(high[:, s], group(highs, g).partition_broadcast(STACK)).then_inc(wide_in[s], 16)
            repeat(sp, STEPS, step)

        @block.vector
        def _(dve):
            dve.tensor_scalar(spare[:], k.iota_p[:], float(NODES_P), None, ALU.add).then_inc(spared, 1)
            dve.wait_ge(spared, 1)

            def matrices(g, s, i):
                mine = k.cols[:, 3, bass.ds(g * TABLES, TABLES)]
                nodes = k.cols[:, 4, bass.ds(g * TABLES, TABLES)]
                wait(dve, mixed, g - 1)
                wait(dve, counts, g - 1)
                dve.wait_ge(wide_in[s], 32 * (i + 1))
                dve.tensor_tensor(same[:, s], wide[:, s], bc(mine.unsqueeze(2), [P, TABLES, P]),
                                  ALU.is_equal).then_inc(sames, 1)
                dve.tensor_tensor(member[:, s], bc(k.iota[:].unsqueeze(1), [P, TABLES, P]),
                                  bc(nodes.unsqueeze(2), [P, TABLES, P]), ALU.is_equal).then_inc(members, 1)
                wait(dve, looked, g - 1)
                dve.tensor_scalar(pick[:, s], high[:, s], k.type_row[:, 0:1], None, ALU.is_equal).then_inc(picks, 1)
                dve.wait_ge(sames, g + 1)
                dve.tensor_tensor(later[:, s], same[:, s], bc(k.upper[:].unsqueeze(1), [P, TABLES, P]),
                                  ALU.mult).then_inc(laters, 1)

            def results(g, r):
                s = r % 2
                mine = k.cols[:, 3, bass.ds(g * TABLES, TABLES)]
                dve.wait_ge(counts, g + 1)
                dve.tensor_scalar(first[:, s], ps_count[:, s, 0:TABLES], 0.0, None, ALU.is_equal).then_inc(firsts, 1)
                dve.wait_ge(firsts, 2 * g + 1)
                dve.scalar_tensor_tensor(first[:, s], mine, spare[:, 0:1], first[:, s], ALU.subtract, ALU.mult).then_inc(firsts, 1)
                dve.wait_ge(firsts, 2 * g + 2)
                wait(dve, sent, g - RING + 1)
                dve.tensor_scalar(place[:, r], first[:, s], spare[:, 0:1], None, ALU.add).then_inc(places, 1)
                dve.wait_ge(looked, g + 1)
                wait(dve, types, g - 1)
                for t in range(TABLES):
                    col = bass.ds(g * TABLES + t, 1)
                    op = dve.scalar_tensor_tensor(junk[:, s, t], k.iota[:], k.cols[:, 2, col], ps_type[:, s, t],
                                                  ALU.is_equal, ALU.mult, accum_out=k.z_type[:, col])
                op.then_inc(types, 1)

            def step(i):
                for r in range(RING):
                    g = RING * i + r
                    matrices(g, r % 2, RING // 2 * i + r // 2)
                    if not (isinstance(g, int) and g == 0):
                        results(g - 1, (r - 1) % RING)
            repeat(dve, STEPS, step)
            results(LAST, LAST % RING)

        @block.tensor
        def _(pe):
            def mixing(g, s):
                pe.wait_ge(members, g + 1)
                wait(pe, mixes, g - 1)
                for t in range(TABLES):
                    mm = pe.matmul(ps_mix[:, s, t, :], member[:, s, t, :], same[:, s, t, :], start=True, stop=True)
                mm.then_inc(mixed, 1)
                pe.wait_ge(picks, g + 1)
                wait(pe, types, g - 1)
                for t in range(TABLES):
                    mm = pe.matmul(ps_type[:, s, t], pick[:, s, t * P:(t + 1) * P], k.type_table[:], start=True, stop=True)
                mm.then_inc(looked, 1)
                pe.wait_ge(laters, g + 1)
                wait(pe, firsts, 2 * (g - 2) + 1)
                for t in range(TABLES):
                    mm = pe.matmul(ps_count[:, s, t:t + 1], later[:, s, t, :], k.onesb[:], start=True, stop=True)
                mm.then_inc(counts, 1)

            def summing(g, s):
                tiles = load_numbers(nc, mybir.EngineType.PE, k.tile_row[0:1, bass.ds(g * TABLES, TABLES)], TILES - 1)
                pe.wait_ge(mixes, g + 1)
                wait(pe, rowed, g - 1)
                for t in range(TABLES):
                    mm = pe.matmul(ps_rows[:, s, t, :], mix[:, s, t, :],
                                   k.u[:, bass.ds(tiles[t], 1), :].squeeze(1), start=True, stop=True)
                mm.then_inc(summed, 1)

            def step(i):
                for r in range(RING):
                    g = RING * i + r
                    mixing(g, r % 2)
                    if not (isinstance(g, int) and g == 0):
                        summing(g - 1, (r - 1) % 2)
            repeat(pe, STEPS, step)
            summing(LAST, LAST % 2)

        @block.scalar
        def _(act):
            def copy_mix(g, s):
                act.wait_ge(mixed, g + 1)
                wait(act, summed, g - 1)
                act.copy(mix[:, s], ps_mix[:, s]).then_inc(mixes, 1)

            def copy_rows(g, r):
                act.wait_ge(summed, g + 1)
                wait(act, sent, g - RING + 1)
                act.copy(rows[:, r], ps_rows[:, r % 2]).then_inc(rowed, 1)

            def step(i):
                for r in range(RING):
                    g = RING * i + r
                    copy_mix(g, r % 2)
                    if not (isinstance(g, int) and g == 0):
                        copy_rows(g - 1, (r - 1) % RING)
            repeat(act, STEPS, step)
            copy_rows(LAST, LAST % RING)

        @block.gpsimd
        def _(pool):
            GROUPS_OF_STEP = 8

            def step(i):
                for q in range(GROUPS_OF_STEP):
                    g, r = GROUPS_OF_STEP * i + q, q % RING
                    pool.wait_ge(places, g + 1)
                    pool.wait_ge(rowed, g + 1)
                    for t in range(TABLES):
                        wait(pool, added[t], 16 * g)
                        pool.sem_inc(turns, 1)
                        pool.indirect_dma_start(k.table_d[t], bass.IndirectOffsetOnAxis(place[:, r, t:t + 1], 0),
                                                rows[:, r, t, :], None, compute_op=ALU.add).then_inc(added[t], 16)
                    if not (isinstance(g, int) and g == 0):
                        pool.sem_inc(sent, 1)
            repeat(pool, ITEMS // TABLES // GROUPS_OF_STEP, step)
            for t in range(TABLES):
                pool.wait_ge(added[t], 16 * ITEMS // TABLES)


def stage_weights1(nc, k, w):
    with ExitStack() as ctx:
        c = Core(nc, ctx)
        fc = c.sb("w_fc", [P, 3, D])
        fc2 = c.sb("w_fc2", [P, 1])
        emb = c.sb("w_emb", [P, RELTILES, D])
        embT = c.sb("w_embT", [P, RELTILES, P])
        rel = c.sb("w_rel", [P, 1, RELTILES])
        rel_parts = c.sb("w_rel_parts", [P, 3, RELTILES], BF16)
        rel_left = c.sb("w_rel_left", [P, 2, RELTILES])
        stack = c.sb("w_stack", [P, STACK])
        step = c.sb("w_step", [STACK, 1])
        vec = c.sb("w_vec", [P, 3])
        psv = c.ps("w_psv", [P, 512])
        pse = c.ps("w_pse", [P, RELTILES, P])
        psr = c.ps("w_psr", [P, 512])
        loaded, prods, taken, zeroed = (c.sem("w_" + s) for s in ("loaded", "prods", "taken", "zeroed"))
        block = ctx.enter_context(nc.Block())

        @block.sync
        def _(sp):
            sp.dma_start(fc[:], w["L1_gnn_attn_fc_w"].rearrange("o (n i) -> o n i", n=3)).then_inc(loaded, 16)
            sp.dma_start(fc2[:], w["L1_gnn_attn_fc2_w"].rearrange("a o -> o a")).then_inc(loaded, 16)
            sp.dma_start(k.w1[:, 0:D], w["L1_gnn_loop_weight"]).then_inc(loaded, 16)
            sp.dma_start(k.wg[:], w["L0_gnn_Wg_w"]).then_inc(loaded, 16)
            sp.wait_ge(zeroed, 1)
            full = RELS // P
            sp.dma_start(emb[:, 0:full, :], w["L1_gnn_emb_rel"][0:full * P, :].rearrange("(t p) d -> p t d", p=P)).then_inc(loaded, 16)
            sp.dma_start(emb[0:RELS - full * P, full, :], w["L1_gnn_emb_rel"][full * P:RELS, :]).then_inc(loaded, 16)

        @block.vector
        def _(dve):
            dve.memset(emb[:, RELS // P, :], 0.0).then_inc(zeroed, 1)
            dve.wait_ge(prods, 1)
            dve.tensor_copy(vec[:], psv[:, 0:3]).then_inc(taken, 1)
            dve.wait_ge(loaded, 16 * 6)
            dve.tensor_copy(k.w1[:, D:D + 2], psv[:, 0:2]).then_inc(taken, 1)
            dve.wait_ge(prods, 2)
            dve.tensor_copy(embT[:], pse[:]).then_inc(taken, 1)
            dve.wait_ge(prods, 3)
            dve.tensor_copy(rel[:, 0], psr[:, 0:RELTILES]).then_inc(taken, 1)
            dve.wait_ge(taken, 4)
            split3(dve, taken, 4, rel_parts[:], rel_left[:], rel[:, 0])
            dve.wait_ge(taken, 9)
            dve.tensor_copy(stack[:], rel_parts[:].rearrange("p a b -> p (a b)")).then_inc(taken, 1)
            dve.wait_ge(prods, 4)
            dve.tensor_copy(k.type_table[:], psr[0:STACK, P:2 * P]).then_inc(taken, 1)
            dve.tensor_scalar(k.type_row[:], k.iota_p[0:STACK], float(RELTILES), -float(RELTILES), ALU.is_ge, ALU.mult).then_inc(taken, 1)
            dve.tensor_scalar(step[:], k.iota_p[0:STACK], float(2 * RELTILES), -float(RELTILES), ALU.is_ge, ALU.mult).then_inc(taken, 1)
            dve.wait_ge(taken, 13)
            dve.tensor_tensor(k.type_row[:], k.type_row[:], step[:], ALU.add).then_inc(taken, 1)
            dve.wait_ge(taken, 14)
            dve.tensor_tensor(k.type_row[:], k.type_row[:], k.iota_p[0:STACK], ALU.add)

        @block.tensor
        def _(pe):
            pe.wait_ge(loaded, 16 * 6)
            for n in range(3):
                mm = pe.matmul(psv[:, n:n + 1], fc[:, n, :], fc2[:], start=True, stop=True)
            mm.then_inc(prods, 1)
            for t in range(RELTILES):
                mm = pe.transpose(pse[:, t, :], emb[:, t, :], k.ident[:])
            mm.then_inc(prods, 1)
            pe.wait_ge(taken, 3)
            for t in range(RELTILES):
                mm = pe.matmul(psr[:, t:t + 1], embT[:, t, :], vec[:, 2:3], start=True, stop=True)
            mm.then_inc(prods, 1)
            pe.wait_ge(taken, 10)
            pe.transpose(psr[0:STACK, P:2 * P], stack[:], k.ident[:]).then_inc(prods, 1)


def split3(dve, link, base, parts, left, whole):
    dve.tensor_copy(parts[:, 0, :], whole).then_inc(link, 1)
    dve.wait_ge(link, base + 1)
    dve.tensor_tensor(left[:, 0, :], whole, parts[:, 0, :], ALU.subtract).then_inc(link, 1)
    dve.wait_ge(link, base + 2)
    dve.tensor_copy(parts[:, 1, :], left[:, 0, :]).then_inc(link, 1)
    dve.wait_ge(link, base + 3)
    dve.tensor_tensor(left[:, 1, :], left[:, 0, :], parts[:, 1, :], ALU.subtract).then_inc(link, 1)
    dve.wait_ge(link, base + 4)
    dve.tensor_copy(parts[:, 2, :], left[:, 1, :]).then_inc(link, 1)


def stage_nodes1(nc, k):
    with ExitStack() as ctx:
        c = Core(nc, ctx)
        xg = c.sb("p_x", [P, 2, G, D])
        pre = c.sb("p_pre", [P, 2, G, D])
        parts = c.sb("p_parts", [P, 2, TABLES, G, D])
        act_in = c.sb("p_act_in", [P, 2, G, D])
        sq = c.sb("p_sq", [P, 2, G, D])
        h = c.sb("p_h", [P, 2, G, D])
        aT = c.sb("p_aT", [P, 2, G, P])
        basis = c.sb("p_basis", [P, 2, G, D])
        sums = c.sb("p_sums", [P, 4, TILES])
        psT = c.ps("p_psT", [P, 8, P])
        psG = c.ps("p_psG", [P, 2, 8, P])
        psL = psG[:].rearrange("p s t d -> p (s t d)").rearrange("p (b f) -> p b f", f=512)
        x_in = [c.sem("p_x_in0"), c.sem("p_x_in1")]
        parts_in = [c.sem("p_parts_in0"), c.sem("p_parts_in1")]
        paired, turned, copied, mult, prepared, gates, x1s, link, centred, squared, varied = (
            c.sem("p_" + s) for s in ("paired", "turned", "copied", "mult", "prepared", "gates", "x1s", "link", "centred",
                                      "squared", "varied"))
        noted, rooted, hs, turned2, copied2, looped, basics, taken = (
            c.sem("p_" + s) for s in ("noted", "rooted", "hs", "turned2", "copied2", "looped", "basics", "taken"))
        h_out = [c.sem("p_h_out0"), c.sem("p_h_out1")]
        b_out = [c.sem("p_b_out0"), c.sem("p_b_out1")]
        block = ctx.enter_context(nc.Block())
        view = lambda d: d.rearrange("(g t p) d -> g p t d", p=P, t=G)
        xv, prev, hv, bv = view(k.x_d), view(k.pre_d), view(k.h1_d), view(k.basis_d)
        tv = [view(k.table_d[t][0:NODES_P, :]) for t in range(TABLES)]
        PAIRS = GROUPS // 2

        def rows_of(g):
            return k.rows[:, bass.ds(g * G, G), :]

        def of(n, g):
            return sums[:, n, bass.ds(g * G, G)]

        def wide(ap):
            return bc(ap.unsqueeze(2), [P, G, D])

        def in_pairs(eng, one, other):
            def step(i):
                one(2 * i, 0, i)
                if not isinstance(i, int):
                    other(2 * i - 1, 1, i - 1)
                one(2 * i + 1, 1, i)
                other(2 * i, 0, i)
            repeat(eng, PAIRS, step)
            other(GROUPS - 1, 1, PAIRS - 1)

        @block.sync
        def _(sp):
            def sums(g, s):
                wait(sp, turned, g - 1)
                for t in range(TABLES):
                    sp.dma_start(parts[:, s, t], group(tv[t], g)).then_inc(parts_in[s], 16)

            def rows(g, s):
                wait(sp, x1s, g - 1)
                sp.dma_start(pre[:, s], group(prev, g)).then_inc(x_in[s], 16)
                sp.dma_start(xg[:, s], group(xv, g)).then_inc(x_in[s], 16)

            in_pairs(sp, lambda g, s, i: sums(g, s), lambda g, s, i: rows(g, s))

        @block.gpsimd
        def _(pool):
            def step(i):
                for s in range(2):
                    g = 2 * i + s
                    pool.wait_ge(parts_in[s], 16 * TABLES * (i + 1))
                    pool.tensor_tensor(parts[:, s, 0:2], parts[:, s, 0:2], parts[:, s, 2:4], ALU.add).then_inc(paired, 1)
            repeat(pool, PAIRS, step)

        @block.vector
        def _(dve):
            def prepare(g, s, i):
                dve.wait_ge(x_in[s], 32 * (i + 1))
                dve.wait_ge(mult, g + 1)
                wait(dve, gates, g - 1)
                dve.tensor_tensor(act_in[:, s], psG[:, s, 0:G], pre[:, s], ALU.add).then_inc(prepared, 1)

            def centre(g, s, i):
                dve.wait_ge(gates, g + 1)
                dve.tensor_tensor(rows_of(g), act_in[:, s], xg[:, s], ALU.add).then_inc(x1s, 1)
                dve.wait_ge(x1s, g + 1)
                dve.tensor_reduce(of(0, g), rows_of(g), AX, ALU.add).then_inc(link, 1)
                dve.wait_ge(link, 2 * g + 1)
                dve.tensor_scalar(of(1, g), of(0, g), -1.0 / D, None, ALU.mult).then_inc(link, 1)
                dve.wait_ge(link, 2 * g + 2)
                dve.tensor_tensor(rows_of(g), rows_of(g), wide(of(1, g)), ALU.add).then_inc(centred, 1)
                if not (isinstance(g, int) and g == 0):
                    spread(g - 1, 1 - s)

            def spread(g, s):
                dve.wait_ge(squared, g + 1)
                dve.sem_inc(noted, 1)
                dve.tensor_reduce(of(2, g), sq[:, s], AX, ALU.add).then_inc(varied, 1)

            in_pairs(dve, prepare, centre)
            spread(GROUPS - 1, 1)
            dve.wait_ge(varied, GROUPS)
            dve.tensor_scalar(sums[:, 0], sums[:, 2], 1.0 / D, EPS, ALU.mult, ALU.add).then_inc(varied, 1)
            dve.wait_ge(rooted, 1)
            dve.reciprocal(sums[:, 2], sums[:, 3]).then_inc(varied, 1)
            dve.wait_ge(varied, GROUPS + 2)

            def scale(g, s, i):
                wait(dve, turned2, g - 1)
                wait(dve, h_out[s], 16 * i)
                dve.scalar_tensor_tensor(h[:, s], rows_of(g), 0.0, wide(of(2, g)), ALU.max, ALU.mult).then_inc(hs, 1)

            def finish(g, s, i):
                dve.wait_ge(looped, g + 1)
                wait(dve, b_out[s], 16 * i)
                for t in range(G):
                    part = psL[:, t // 3, (t % 3) * (D + 2):(t % 3 + 1) * (D + 2)]
                    dve.scalar_tensor_tensor(basis[:, s, t], part[:, 0:D], sums[:, 1, bass.ds(g * G + t, 1)],
                                             k.rows[:, bass.ds(g * G + t, 1), :].squeeze(1),
                                             ALU.subtract, ALU.add).then_inc(basics, 1)
                for a, n in ((0, 3), (3, 3), (6, 1)):
                    part = psL[:, a // 3, 0:n * (D + 2)].rearrange("p (t d) -> p t d", t=n)
                    for m in range(2):
                        mv = dve.tensor_copy(k.node_scores[:, m, bass.ds(g * G + a, n)], part[:, :, D + m])
                mv.then_inc(taken, 1)

            def step(i):
                for s in range(2):
                    g = 2 * i + s
                    if not (isinstance(g, int) and g == GROUPS - 1):
                        scale(g + 1, 1 - s, i + s)
                    if not (isinstance(g, int) and g == 0):
                        finish(g - 1, 1 - s, i if s else i - 1)
            scale(0, 0, 0)
            repeat(dve, PAIRS - 1, step)
            step(PAIRS - 1)
            finish(GROUPS - 1, 1, PAIRS - 1)

        @block.tensor
        def _(pe):
            def turn(g, s, i):
                pe.wait_ge(paired, g + 1)
                wait(pe, copied, g)
                for t in range(G):
                    for q in range(2):
                        mm = pe.matmul(psT[:, t, :], parts[:, s, q, t, :], k.ident[:], start=(q == 0), stop=(q == 1))
                mm.then_inc(turned, 1)

            def product(g, s, i):
                pe.wait_ge(copied, g + 1)
                wait(pe, prepared, g - 1)
                for t in range(G):
                    mm = pe.matmul(psG[:, s, t, :], aT[:, s, t, :], k.wg[:], start=True, stop=True)
                mm.then_inc(mult, 1)

            in_pairs(pe, turn, product)

            def turn2(g, s, i):
                pe.wait_ge(hs, g + 1)
                wait(pe, copied2, g)
                for t in range(G):
                    mm = pe.transpose(psT[:, t, :], h[:, s, t, :], k.ident[:])
                mm.then_inc(turned2, 1)

            def product2(g, s, i):
                pe.wait_ge(copied2, g + 1)
                wait(pe, taken, g)
                for t in range(G):
                    at = (t % 3) * (D + 2)
                    mm = pe.matmul(psL[:, t // 3, at:at + D + 2], aT[:, s, t, :], k.w1[:], start=True, stop=True)
                mm.then_inc(looped, 1)

            in_pairs(pe, turn2, product2)

        @block.scalar
        def _(act):
            def copy(g, s, i):
                act.wait_ge(turned, g + 1)
                wait(act, mult, g - 1)
                act.copy(aT[:, s], psT[:, 0:G]).then_inc(copied, 1)

            def gate(g, s, i):
                act.wait_ge(prepared, g + 1)
                act.activation(act_in[:, s], act_in[:, s], ACT.Tanh).then_inc(gates, 1)
                if not (isinstance(g, int) and g == 0):
                    square(g - 1, 1 - s)

            def square(g, s):
                act.wait_ge(centred, g + 1)
                wait(act, varied, g)
                act.activation(sq[:, s], rows_of(g), ACT.Square).then_inc(squared, 1)

            in_pairs(act, copy, gate)
            square(GROUPS - 1, 1)
            act.wait_ge(varied, GROUPS + 1)
            act.activation(sums[:, 3], sums[:, 0], ACT.Sqrt).then_inc(rooted, 1)

            def copy2(g, s, i):
                act.wait_ge(hs, g + 1)
                act.dma_start(group(hv, g), h[:, s]).then_inc(h_out[s], 16)
                act.wait_ge(turned2, g + 1)
                wait(act, looped, g - 1)
                act.copy(aT[:, s], psT[:, 0:G]).then_inc(copied2, 1)

            def store(g, s, i):
                act.wait_ge(basics, G * g + G)
                act.dma_start(group(bv, g), basis[:, s]).then_inc(b_out[s], 16)

            in_pairs(act, copy2, store)
            for s in range(2):
                act.wait_ge(h_out[s], 16 * PAIRS)
                act.wait_ge(b_out[s], 16 * PAIRS)


def stage_scores(nc, k):
    with ExitStack() as ctx:
        c = Core(nc, ctx)
        wide_src = c.sb("z_wide_src", [TILES, 2, ZSRC * P], BF16)
        wide_dst = c.sb("z_wide_dst", [P, 2, ZDST * P], BF16)
        pick = c.sb("z_pick", [TILES, 2, ZSRC * P], BF16)
        member = c.sb("z_member", [P, 2, ZDST * P], BF16)
        junk = c.sb("z_junk", [P, 4, P])
        z_src = c.sb("z_src", [P, ROWS])
        tile_wide = c.sb("z_tile_wide", [TILES, ITEMS], I32)
        tile_pick = c.sb("z_tile_pick", [TILES, ITEMS], BF16)
        dst_parts = c.sb("z_dst_parts", [P, ITEMS, 3], BF16)
        score_rows = c.sb("z_score_rows", [TILES, P])
        asked = c.sb("z_asked", [P, 2, ZP], I32)
        got = c.sb("z_got", [P, 2, ZP])
        scores_out, asks, gots, fetched, turns = (
            c.sem("z_" + s) for s in ("scores_out", "asks", "gots", "fetched", "turns"))
        got_in = [c.sem("z_got_in0"), c.sem("z_got_in1")]
        z_dst3 = c.sb("z_dst3", [P, ITEMS, 3])
        dst_left = z_dst3[:].rearrange("p i m -> p (i m)")[:, 0:2 * ITEMS].rearrange("p (m i) -> p m i", m=2)
        z_dst = c.sb("z_dst", [P, ITEMS])
        z_dstT = c.sb("z_dstT", [P, BLOCKS, P])
        chunk_f = c.sb("z_chunk_f", [P, BLOCKS])
        move = c.sb("z_move", [P, 2 * BLOCKS, P])
        zt = c.sb("z_zt", [P, BLOCKS, P])
        psT = c.ps("z_psT", [P, 512])
        psA = c.ps("z_psA", [P, 4, 512])
        psD = c.ps("z_psD", [P, 2, 512])
        wide_in = [c.sem("z_wide_in0"), c.sem("z_wide_in1")]
        dst_in = [c.sem("z_dst_in0"), c.sem("z_dst_in1")]
        distances = c.sem("z_distances")
        minus_p = c.sb("z_minus_p", [P, 1])
        turned, link, columns, picks, members, looked, found, zs, taken = (
            c.sem("z_" + s) for s in ("turned", "link", "columns", "picks", "members", "looked", "found", "zs", "taken"))
        tiles_in, rows_of_z, copied, moves, out, back = (
            c.sem("z_" + s) for s in ("tiles_in", "rows_of_z", "copied", "moves", "out", "back"))
        block = ctx.enter_context(nc.Block())
        hv = k.high_d[0][0:ZG * ZSRC, :].rearrange("(g c) e -> g (c e)", c=ZSRC)
        dv = k.item_dst_d.rearrange("(g c) e -> g (c e)", c=ZDST)
        STEPS = ZG // 2
        SRC_CHUNKS = ZG * ZSRC
        assert ZG * ZDST == ROWS and 2 * ZSRC % 4 == 0
        quarters = [(a, min(a + 512, ITEMS)) for a in range(0, ITEMS, 512)]

        @block.sync
        def _(sp):
            sp.dma_start(tile_wide[:], k.tile_d.partition_broadcast(TILES)).then_inc(tiles_in, 16)
            sp.wait_ge(link, 1)
            sp.dma_start(k.src_score_d.rearrange("(t p) a -> t (p a)", p=P), score_rows[:]).then_inc(scores_out, 16)

            def step(i):
                for s in range(2):
                    g = 2 * i + s
                    wait(sp, picks, g - 1)
                    wait(sp, members, g - 1)
                    sp.dma_start(wide_src[:, s], group(hv, g).partition_broadcast(TILES)).then_inc(wide_in[s], 16)
                    sp.dma_start(wide_dst[:, s], group(dv, g).partition_broadcast(P)).then_inc(dst_in[s], 16)
            repeat(sp, STEPS, step)
            sp.wait_ge(back, BLOCKS)
            sp.dma_start(k.z_d.rearrange("(b p) e -> p b e", p=P), zt[:]).then_inc(out, 16)
            sp.wait_ge(out, 16)

        @block.vector
        def _(dve):
            dve.wait_ge(turned, 2)
            dve.memset(z_src[:, SRC_CHUNKS + ZP_GROUPS * ZP:ROWS], 0.0)
            dve.tensor_copy(score_rows[:], psT[0:TILES, 0:P]).then_inc(link, 1)
            for n in range(2):
                split3(dve, link, 5 * n + 1, k.parts[0:TILES, n], k.split[0:TILES, n], psT[0:TILES, n * P:(n + 1) * P])
            dve.wait_ge(tiles_in, 16)
            dve.tensor_scalar(tile_pick[:], tile_wide[:], k.iota_p[0:TILES, 0:1], None, ALU.is_equal).then_inc(link, 1)
            dve.wait_ge(columns, 1)
            flat = psA[:].rearrange("p b f -> p (b f)")[:, 0:ITEMS]
            dve.tensor_copy(dst_parts[:, :, 0], flat).then_inc(link, 1)
            dve.wait_ge(link, 13)
            dve.tensor_tensor(dst_left[:, 0], flat, dst_parts[:, :, 0], ALU.subtract).then_inc(link, 1)
            dve.wait_ge(link, 14)
            dve.tensor_copy(dst_parts[:, :, 1], dst_left[:, 0]).then_inc(link, 1)
            dve.wait_ge(link, 15)
            dve.tensor_tensor(dst_left[:, 1], dst_left[:, 0], dst_parts[:, :, 1], ALU.subtract).then_inc(link, 1)
            dve.wait_ge(link, 16)
            dve.tensor_copy(dst_parts[:, :, 2], dst_left[:, 1]).then_inc(link, 1)
            dve.tensor_scalar(minus_p[:], k.iota_p[:], -1.0, None, ALU.mult).then_inc(link, 1)

            def masks(g, s, i):
                dve.wait_ge(wide_in[s], 16 * (i + 1))
                wait(dve, looked, (g - 1) * ZSRC)
                dve.tensor_scalar(pick[:, s], wide_src[:, s], k.iota_p[0:TILES, 0:1], None, ALU.is_equal).then_inc(picks, 1)

            def choose(g, s, i):
                for j in range(ZSRC):
                    bank = (s * ZSRC + j) % 4
                    dve.wait_ge(looked, g * ZSRC + j + 1)
                    wait(dve, zs, g * ZSRC + j - 3)
                    col = bass.ds(g * ZSRC + j, 1)
                    dve.scalar_tensor_tensor(junk[:, bank, :], k.iota[:], k.cols[:, 0, col],
                                             psA[:, bank, 0:P], ALU.is_equal, ALU.mult,
                                             accum_out=z_src[:, col]).then_inc(zs, 1)

            def step(i):
                masks(2 * i, 0, i)
                if not isinstance(i, int):
                    choose(2 * i - 1, 1, i - 1)
                masks(2 * i + 1, 1, i)
                choose(2 * i, 0, i)
            repeat(dve, STEPS, step)
            choose(2 * STEPS - 1, 1, STEPS - 1)
            dve.wait_ge(zs, SRC_CHUNKS)
            dve.wait_ge(fetched, 1)
            dve.tensor_tensor(z_src[:], z_src[:], k.z_type[:], ALU.add).then_inc(rows_of_z, 1)
            dve.wait_ge(taken, 2 * STEPS)
            dve.tensor_reduce(z_dst[:], z_dst3[:], AX, ALU.add).then_inc(rows_of_z, 1)
            dve.tensor_copy(chunk_f[:], k.chunk_of[:]).then_inc(moves, 1)
            for b in range(BLOCKS):
                for m in range(2):
                    if b + m < BLOCKS:
                        dve.wait_ge(moves, 1)
                        dve.tensor_scalar(move[:, 2 * b + m], k.iota[:], float(b * P), chunk_f[:, b + m:b + m + 1],
                                          ALU.add, ALU.is_equal).then_inc(moves, 1)

        @block.gpsimd
        def _(pool):
            def ask(n, s, i):
                wait(pool, got_in[s], 16 * ZP * i)
                pool.tensor_copy(asked[:, s], k.cols[:, 1, bass.ds(n * ZP + SRC_CHUNKS, ZP)]).then_inc(asks, 1)
                pool.wait_ge(asks, n + 1)
                wait(pool, gots, n - 1)
                pool.sem_inc(turns, 1)
                for j in range(ZP):
                    pool.indirect_dma_start(got[:, s, j:j + 1], None, k.src_score_d[:],
                                            bass.IndirectOffsetOnAxis(asked[:, s, j:j + 1], 0)).then_inc(got_in[s], 16)

            def take(n, s, i):
                pool.wait_ge(got_in[s], 16 * ZP * (i + 1))
                pool.tensor_copy(z_src[:, bass.ds(n * ZP + SRC_CHUNKS, ZP)], got[:, s]).then_inc(gots, 1)

            def step(i):
                for s in range(2):
                    n = 2 * i + s
                    ask(n, s, i)
                    if not (isinstance(n, int) and n == 0):
                        take(n - 1, 1 - s, i if s else i - 1)
            pool.wait_ge(scores_out, 16)
            repeat(pool, ZP_GROUPS // 2, step)
            take(ZP_GROUPS - 1, 1, ZP_GROUPS // 2 - 1)
            pool.wait_ge(gots, ZP_GROUPS)
            pool.sem_inc(fetched, 1)

        @block.tensor
        def _(pe):
            for n in range(2):
                pe.transpose(psT[0:TILES, n * P:(n + 1) * P], k.node_scores[:, n, :], k.ident[:]).then_inc(turned, 1)
            pe.wait_ge(link, 12)
            for q, (a, b) in enumerate(quarters):
                for m in range(3):
                    mm = pe.matmul(psA[:, q, 0:b - a], k.parts[0:TILES, 1, m, :], tile_pick[:, a:b],
                                   start=(m == 0), stop=(m == 2))
            mm.then_inc(columns, 1)
            pe.wait_ge(link, 18)

            def step(i):
                for s in range(2):
                    g = 2 * i + s
                    pe.wait_ge(picks, g + 1)
                    for j in range(ZSRC):
                        wait(pe, zs, g * ZSRC + j - 3)
                        for m in range(3):
                            mm = pe.matmul(psA[:, (s * ZSRC + j) % 4, 0:P], pick[:, s, j * P:(j + 1) * P],
                                           k.parts[0:TILES, 0, m, :], start=(m == 0), stop=(m == 2))
                        mm.then_inc(looked, 1)
                        if j == 1:
                            pe.wait_ge(members, g + 1)
                            wait(pe, taken, g - 1)
                        if j >= 1:
                            for d in range((j - 1) * ZDST // (ZSRC - 1), j * ZDST // (ZSRC - 1)):
                                mm = dst_part(g, s, d)
                    mm.then_inc(found, 1)

            def dst_part(g, s, j):
                return pe.matmul(psD[:, s, 3 * j:3 * j + 3], member[:, s, j * P:(j + 1) * P],
                                 dst_parts[:, bass.ds(g * ZDST + j, 1), :].squeeze(1), start=True, stop=True)

            repeat(pe, STEPS, step)
            pe.wait_ge(rows_of_z, 2)
            for q, b0 in enumerate(range(0, BLOCKS, 4)):
                for b in range(b0, min(b0 + 4, BLOCKS)):
                    at = (b - b0) * P
                    mm = pe.transpose(psA[:, q, at:at + P], z_dst[:, b * P:(b + 1) * P], k.ident[:])
                mm.then_inc(turned, 1)
            pe.wait_ge(copied, 4)
            pe.wait_ge(moves, 2 * BLOCKS)
            for b in range(BLOCKS):
                if b >= 2:
                    pe.wait_ge(back, b - 1)
                last = min(2, BLOCKS - b)
                pe.matmul(psD[:, b % 2, 0:P], z_src[:, b * P:(b + 1) * P], k.ident[:], start=True, stop=False)
                for m in range(last):
                    mm = pe.matmul(psD[:, b % 2, 0:P], move[:, 2 * b + m], z_dstT[:, b + m], start=False, stop=(m == last - 1))
                mm.then_inc(moves, 1)

        @block.scalar
        def _(act):
            def masks(g, s, i):
                act.wait_ge(dst_in[s], 16 * (i + 1))
                wait(act, found, g - 1)
                act.activation(member[:, s], wide_dst[:, s], ACT.Abs, bias=minus_p[:]).then_inc(distances, 1)
                act.wait_ge(distances, g + 1)
                act.activation(member[:, s], member[:, s], ACT.Relu, bias=k.ones[:, 0:1], scale=-1.0).then_inc(members, 1)

            def take(g, s, i):
                act.wait_ge(found, g + 1)
                act.copy(z_dst3[:, bass.ds(g * ZDST, ZDST), :].rearrange("p a b -> p (a b)"), psD[:, s, 0:3 * ZDST]).then_inc(taken, 1)

            def step(i):
                masks(2 * i, 0, i)
                if not isinstance(i, int):
                    take(2 * i - 1, 1, i - 1)
                masks(2 * i + 1, 1, i)
                take(2 * i, 0, i)
            act.wait_ge(link, 18)
            repeat(act, STEPS, step)
            take(2 * STEPS - 1, 1, STEPS - 1)
            for q, b0 in enumerate(range(0, BLOCKS, 4)):
                m = min(4, BLOCKS - b0)
                act.wait_ge(turned, q + 3)
                act.copy(z_dstT[:, b0:b0 + m, :].rearrange("p b e -> p (b e)"), psA[:, q, 0:m * P]).then_inc(copied, 1)
            for b in range(BLOCKS):
                act.wait_ge(moves, 2 * BLOCKS + b + 1)
                act.copy(zt[:, b], psD[:, b % 2, 0:P]).then_inc(back, 1)


def stage_softmax(nc, k):
    with ExitStack() as ctx:
        c = Core(nc, ctx)
        dstp = c.sb("s_dst", [P, SCAN])
        before = c.sb("s_before", [P, 1])
        after = c.sb("s_after", [P, 1])
        z = c.sb("s_z", [P, SCAN])
        cut = c.sb("s_cut", [P, SCAN + 1])
        top = c.sb("s_top", [P, SCAN])
        top2 = c.sb("s_top2", [P, SCAN])
        ends = c.sb("s_ends", [P, 2])
        rowsT = c.sb("s_rowsT", [1, 2, P])
        carry = c.sb("s_carry", [1, P + 1])
        colc = c.sb("s_colc", [P, 1])
        wts = c.sb("s_wts", [P, BLOCKS, P])
        zero = c.sb("s_zero", [P, P])
        psA = c.ps("s_psA", [P, 512])
        psB = c.ps("s_psB", [P, 512])
        psW = c.ps("s_psW", [P, 4, 512])
        loaded, sent, link, turned, moved, exped = (c.sem("s_" + s) for s in ("loaded", "sent", "link", "turned", "moved", "exped"))
        out, gathered, wT, wc = (c.sem("s_" + s) for s in ("out", "gathered", "wT", "wc"))
        block = ctx.enter_context(nc.Block())
        N = P * SCAN
        flat = lambda d: d.rearrange("r e -> (r e)")
        runs = lambda d: flat(d)[0:N].rearrange("(p j) -> p j", p=P)

        @block.sync
        def _(sp):
            sp.wait_ge(sent, 3)
            sp.dma_start(dstp[:], runs(k.dst_d)).then_inc(loaded, 16)
            sp.dma_start(z[:], runs(k.z_d)).then_inc(loaded, 16)
            nxt = runs(k.dst_d)
            with nc.allow_non_contiguous_dma("127 single numbers"):
                sp.dma_start(before[1:P, :], nxt[0:P - 1, SCAN - 1:SCAN]).then_inc(loaded, 16)
                sp.dma_start(after[0:P - 1, :], nxt[1:P, 0:1]).then_inc(loaded, 16)
            sp.dma_start(flat(k.w_d)[N:ROWS * P].rearrange("(p j) -> p j", j=P), zero[0:ROWS - CHUNKS, :]).then_inc(out, 16)
            sp.wait_ge(exped, 1)
            sp.dma_start(runs(k.w_d), top[:]).then_inc(out, 16)

        @block.vector
        def _(dve):
            n = [0]

            def link_up(op):
                n[0] += 1
                op.then_inc(link, 1)
                dve.wait_ge(link, n[0])

            dve.memset(before[:], -1.0).then_inc(sent, 1)
            dve.memset(after[:], -1.0).then_inc(sent, 1)
            dve.memset(zero[:], 0.0).then_inc(sent, 1)
            dve.wait_ge(loaded, 64)
            link_up(dve.tensor_tensor(cut[:, 1:SCAN], dstp[:, 1:SCAN], dstp[:, 0:SCAN - 1], ALU.not_equal))
            link_up(dve.tensor_tensor(cut[:, 0:1], dstp[:, 0:1], before[:], ALU.not_equal))
            link_up(dve.tensor_tensor(cut[:, SCAN:], dstp[:, SCAN - 1:], after[:], ALU.not_equal))
            link_up(dve.tensor_scalar(cut[:], cut[:], LOW, None, ALU.mult))
            link_up(dve.scalar_tensor_tensor(z[:], z[:], SLOPE, z[:], ALU.mult, ALU.max))

            for turn in range(2):
                a = z if turn == 0 else top
                b = top if turn == 0 else top2
                data = a[:] if turn == 0 else a[:, ::-1]
                outp = b[:] if turn == 0 else b[:, ::-1]
                gaps = cut[:, 0:SCAN] if turn == 0 else cut[:, SCAN:0:-1]
                link_up(dve.tensor_tensor_scan(outp, gaps, data, LOW, ALU.add, ALU.max))
                end = b[:, SCAN - 1:SCAN] if turn == 0 else b[:, 0:1]
                link_up(dve.tensor_copy(ends[:, 0:1], end))
                link_up(dve.tensor_reduce(ends[:, 1:2], gaps, AX, ALU.min))
                dve.wait_ge(turned, turn + 1)
                link_up(dve.tensor_copy(rowsT[:, 0], psA[0:1, 0:P]))
                link_up(dve.tensor_copy(rowsT[:, 1], psA[0:1, P:2 * P]))
                link_up(dve.memset(carry[:], LOW))
                if turn == 0:
                    link_up(dve.tensor_tensor_scan(carry[:, 1:P + 1], rowsT[:, 1], rowsT[:, 0], LOW, ALU.add, ALU.max))
                    use = carry[:, 0:P]
                else:
                    link_up(dve.tensor_tensor_scan(carry[:, 0:P][:, ::-1], rowsT[:, 1][:, ::-1], rowsT[:, 0][:, ::-1],
                                                   LOW, ALU.add, ALU.max))
                    use = carry[:, 1:P + 1]
                link_up(dve.tensor_copy(rowsT[:, 0], use))
                dve.wait_ge(moved, turn + 1)
                link_up(dve.tensor_copy(colc[:, 0:1], psB[:, 0:1]))
                link_up(dve.tensor_tensor_scan(outp, gaps, data, colc[:, 0:1], ALU.add, ALU.max))
            link_up(dve.tensor_tensor(z[:], z[:], top2[:], ALU.subtract))
            for b0 in range(0, BLOCKS, 4):
                m = min(4, BLOCKS - b0)
                dve.wait_ge(wT, b0 // 4 + 1)
                dve.tensor_copy(k.wcol[:, b0 * P:(b0 + m) * P], psW[:, b0 // 4, 0:m * P]).then_inc(wc, 1)

        STEPS_A = 5
        PER = 11

        @block.tensor
        def _(pe):
            for turn in range(2):
                pe.wait_ge(link, STEPS_A + turn * (PER - 1) + 3)
                pe.transpose(psA[0:1, 0:P], ends[:, 0:1], k.ident[:])
                pe.transpose(psA[0:1, P:2 * P], ends[:, 1:2], k.ident[:]).then_inc(turned, 1)
                pe.wait_ge(link, STEPS_A + turn * (PER - 1) + 8)
                pe.transpose(psB[:, 0:1], rowsT[0:1, 0, :], k.ident[0:1, 0:1]).then_inc(moved, 1)
            pe.wait_ge(gathered, 16 * BLOCKS)
            for b0 in range(0, BLOCKS, 4):
                for b in range(b0, min(b0 + 4, BLOCKS)):
                    at = (b - b0) * P
                    mm = pe.transpose(psW[:, b0 // 4, at:at + P], wts[:, b, :], k.ident[:])
                mm.then_inc(wT, 1)

        @block.scalar
        def _(act):
            act.wait_ge(link, STEPS_A + 2 * (PER - 1) + 1)
            act.activation(top[:], z[:], ACT.Exp).then_inc(exped, 1)

        @block.gpsimd
        def _(pool):
            pool.wait_ge(out, 32)
            for b in range(BLOCKS):
                pool.indirect_dma_start(wts[:, b, :], None, k.w_d[:],
                                        bass.IndirectOffsetOnAxis(k.chunk_of[:, b:b + 1], 0)).then_inc(gathered, 16)


def stage_messages1(nc, k):
    with ExitStack() as ctx:
        c = Core(nc, ctx)
        SLOTS = 8
        place = c.sb("g_place", [P, 2, SLOTS], I32)
        rows = c.sb("g_rows", [P, SLOTS, D + 1])
        member = c.sb("g_member", [P, SLOTS, P])
        away = c.sb("g_away", [P, 2, P])
        minus_w = c.sb("g_minus_w", [P, ITEMS])
        distances = c.sem("g_distances")
        ps = c.ps("g_ps", [P, SLOTS, 512])
        ones, places, members, added, readied = (c.sem("g_" + s) for s in ("ones", "places", "members", "added", "readied"))
        summed, turns = c.sem("g_summed"), c.sem("g_turns")
        row_in = [c.sem(f"g_row_in{j}") for j in range(SLOTS)]
        block = ctx.enter_context(nc.Block())
        STEPS = ITEMS // SLOTS // 2

        @block.gpsimd
        def _(pool):
            pool.memset(rows[:, :, D:D + 1], 1.0).then_inc(ones, 1)

            GROUPS_OF_STEP = 4

            def step(i):
                for q in range(GROUPS_OF_STEP):
                    g, s = GROUPS_OF_STEP * i + q, q % 2
                    pool.wait_ge(places, g + 1)
                    for j in range(SLOTS):
                        wait(pool, summed, SLOTS * (g - 1) + j + 1)
                        pool.sem_inc(turns, 1)
                        pool.indirect_dma_start(rows[:, j, 0:D], None, k.h1_d[:],
                                                bass.IndirectOffsetOnAxis(place[:, s, j:j + 1], 0)
                                                ).then_inc(row_in[j], 16)
            repeat(pool, ITEMS // SLOTS // GROUPS_OF_STEP, step)

        @block.scalar
        def _(act):
            def step(i):
                for s in range(2):
                    g = 2 * i + s
                    wait(act, summed, SLOTS * (g - 1))
                    act.copy(place[:, s], k.place_col[:, bass.ds(g * SLOTS, SLOTS)]).then_inc(places, 1)
                    for j in range(SLOTS):
                        it = g * SLOTS + j
                        act.activation(away[:, j % 2], k.iota[:], ACT.Abs, scale=-1.0,
                                       bias=k.cols[:, 4, bass.ds(it, 1)]).then_inc(distances, 1)
                        wait(act, summed, SLOTS * (g - 1) + j + 1)
                        act.wait_ge(distances, it + 1)
                        act.activation(member[:, j], away[:, j % 2], ACT.Relu, scale=minus_w[:, bass.ds(it, 1)],
                                       bias=k.wcol[:, bass.ds(it, 1)]).then_inc(members, 1)
            act.wait_ge(readied, 2)
            repeat(act, STEPS, step)

        @block.vector
        def _(dve):
            def step(i):
                for s in range(2):
                    g = 2 * i + s
                    tiles = load_numbers(nc, mybir.EngineType.DVE, k.tile_row[0:1, bass.ds(g * SLOTS, SLOTS)], TILES - 1)
                    for j in range(SLOTS):
                        it = g * SLOTS + j
                        tile = tiles[j]
                        dve.wait_ge(summed, it + 1)
                        wait(dve, added, it)
                        acc = k.acc[:, bass.ds(tile, 1), :].squeeze(1)
                        dve.tensor_tensor(acc, acc, ps[:, j, 0:D + 1], ALU.add).then_inc(added, 1)
            dve.tensor_scalar(minus_w[:], k.wcol[:], -1.0, None, ALU.mult).then_inc(readied, 1)
            dve.memset(k.acc[:], 0.0).then_inc(readied, 1)
            dve.wait_ge(readied, 2)
            repeat(dve, STEPS, step)

        @block.tensor
        def _(pe):
            pe.wait_ge(ones, 1)

            def step(i):
                for s in range(2):
                    g = 2 * i + s
                    for j in range(SLOTS):
                        it = g * SLOTS + j
                        pe.wait_ge(row_in[j], 16 * (g + 1))
                        pe.wait_ge(members, it + 1)
                        wait(pe, added, it - SLOTS + 1)
                        pe.matmul(ps[:, j, 0:D + 1], member[:, j, :], rows[:, j, :], start=True, stop=True).then_inc(summed, 1)
            repeat(pe, STEPS, step)


def stage_out(nc, k, out):
    with ExitStack() as ctx:
        c = Core(nc, ctx)
        basis = c.sb("o_basis", [P, 2, G, D])
        mean = c.sb("o_mean", [P, G, D])
        den = c.sb("o_den", [P, 2, TILES])
        res = c.sb("o_res", [P, 2, G, D])
        b_in = [c.sem("o_b_in0"), c.sem("o_b_in1")]
        r_out = [c.sem("o_r_out0"), c.sem("o_r_out1")]
        dens, means, sums = (c.sem("o_" + s) for s in ("dens", "means", "sums"))
        block = ctx.enter_context(nc.Block())
        bv = k.basis_d.rearrange("(g t p) d -> g p t d", p=P, t=G)
        ov = out[0:(GROUPS - 1) * G * P, :].rearrange("(g t p) d -> g p t d", p=P, t=G)
        tail = out[(GROUPS - 1) * G * P:, :]
        left = NODES - (GROUPS - 1) * G * P
        m = left // P

        @block.sync
        def _(sp):
            for g in range(GROUPS):
                if g >= 2:
                    sp.wait_ge(sums, g - 1)
                sp.dma_start(basis[:, g % 2], bv[g]).then_inc(b_in[g % 2], 16)

        @block.vector
        def _(dve):
            dve.tensor_scalar(den[:, 0], k.acc[:, :, D], 1e-30, None, ALU.max).then_inc(dens, 1)
            dve.wait_ge(dens, 1)
            dve.reciprocal(den[:, 1], den[:, 0]).then_inc(dens, 1)
            dve.wait_ge(dens, 2)
            for g in range(GROUPS):
                dve.wait_ge(b_in[g % 2], 16 * (g // 2 + 1))
                if g >= 1:
                    dve.wait_ge(sums, g)
                dve.tensor_tensor(mean[:], k.acc[:, g * G:(g + 1) * G, 0:D],
                                  bc(den[:, 1, g * G:(g + 1) * G].unsqueeze(2), [P, G, D]), ALU.mult).then_inc(means, 1)
                dve.wait_ge(means, g + 1)
                if g >= 2:
                    dve.wait_ge(r_out[g % 2], 16 * (g // 2))
                dve.tensor_tensor(res[:, g % 2], mean[:], basis[:, g % 2], ALU.add).then_inc(sums, 1)

        @block.scalar
        def _(act):
            for g in range(GROUPS - 1):
                act.wait_ge(sums, g + 1)
                act.dma_start(ov[g], res[:, g % 2]).then_inc(r_out[g % 2], 16)
            s = (GROUPS - 1) % 2
            act.wait_ge(sums, GROUPS)
            act.dma_start(tail[0:m * P, :].rearrange("(t p) d -> p t d", p=P), res[:, s, 0:m]).then_inc(r_out[s], 16)
            act.dma_start(tail[m * P:left, :], res[0:left - m * P, s, m]).then_inc(r_out[s], 16)
            act.wait_ge(r_out[0], 16 * 7 + (16 if s == 0 else 0))
            act.wait_ge(r_out[1], 16 * 7 + (16 if s == 1 else 0))


class Kept:
    pass


def build(nc, x, src, dst, typ, w, out):
    k = Kept()
    k.src_d = nc.dram_tensor("src_rows", [ROWS, P], F32).ap()
    k.dst_d = nc.dram_tensor("dst_rows", [ROWS, P], F32).ap()
    k.high_d = nc.dram_tensor("high_digits", [3, ROWS, P], BF16).ap()
    k.item_src_d = nc.dram_tensor("item_src", [ITEMS, P], F32).ap()
    k.item_dst_d = nc.dram_tensor("item_dst", [ITEMS, P], BF16).ap()
    k.tile_d = nc.dram_tensor("item_tiles", [ITEMS], I32).ap()
    k.x_d = nc.dram_tensor("x_rows", [NODES_P, D], F32).ap()
    k.pre_d = nc.dram_tensor("pre_rows", [NODES_P, D], F32).ap()
    k.h1_d = nc.dram_tensor("h1_rows", [NODES_P, D], F32).ap()
    k.basis_d = nc.dram_tensor("basis_rows", [NODES_P, D], F32).ap()
    k.z_d = nc.dram_tensor("z_rows", [ROWS, P], F32).ap()
    k.w_d = nc.dram_tensor("w_rows", [ROWS, P], F32).ap()
    k.src_score_d = nc.dram_tensor("src_scores", [NODES_P, 1], F32).ap()
    k.table_d = [nc.dram_tensor(f"sum_table{t}", [TABLE, D], F32).ap() for t in range(TABLES)]
    with ExitStack() as ctx:
        c = Core(nc, ctx)
        k.ident = c.sb("ident", [P, P])
        k.upper = c.sb("upper", [P, P], BF16)
        k.ones = c.sb("ones", [P, P])
        k.onesb = c.sb("onesb", [P, 1], BF16)
        k.iota = c.sb("iota", [P, P])
        k.iota_p = c.sb("iota_p", [P, 1])
        k.cols = c.sb("cols", [P, 5, ROWS])
        k.tile_row = c.sb("tile_row", [1, ITEMS], I32)
        k.place_col = c.sb("place_cols", [P, ITEMS], I32)
        k.z_type = c.sb("z_type", [P, ROWS])
        k.chunk_of = c.sb("chunk_of", [P, BLOCKS], I32)
        k.node_scores = c.sb("node_scores", [P, 2, TILES])
        k.parts = c.sb("table_parts", [TILES, 2, 3, P], BF16)
        k.split = c.sb("table_split", [TILES, 2, 2, P])
        k.type_table = c.sb("type_table", [STACK, P], BF16)
        k.type_row = c.sb("type_row", [STACK, 1])
        k.w1 = c.sb("w1", [P, D + 2])
        k.wg = c.sb("wg", [P, D])
        stage_constants(nc, k)
        with ExitStack() as inner:
            q = Core(nc, inner)
            k.raw = q.sb("raw_edges", [P, 3, BLOCKS, P], I32)
            k.unsorted = q.sb("unsorted", [1, 1], I32)
            stage_load(nc, k, src, dst, typ)
            unsorted = nc.values_load(k.unsorted[:], min_val=0, max_val=1)
            with nc.If(unsorted > 0):
                stage_sort(nc, k)
            stage_edges(nc, k)
        stage_weights1(nc, k, w)
        with ExitStack() as inner:
            k.u = k.rows = Core(nc, inner).sb("node_rows", [P, TILES, D])
            stage_nodes0(nc, k, x, w)
            stage_messages0(nc, k)
            stage_nodes1(nc, k)
        stage_scores(nc, k)
        k.wcol = c.sb("w_cols", [P, ITEMS])
        stage_softmax(nc, k)
        k.acc = c.sb("acc", [P, TILES, D + 1])
        stage_messages1(nc, k)
        stage_out(nc, k, out)
    return nc


_EDGE = ("src", "dst", "edge_type_460")


def kernel(**inputs):
    import numpy as _np
    import concourse.bacc as _bacc
    from concourse import mybir as _mybir
    from concourse.bass_utils import run_bass_kernel_spmd as _run

    nc = _bacc.Bacc("TRN2", target_bir_lowering=False, num_devices=1)
    arrays, args = {}, {}
    for name in inputs:
        a = _np.ascontiguousarray(inputs[name])
        arrays[f"in_{name}"] = a
        args[name] = nc.dram_tensor(f"in_{name}", a.shape, _mybir.dt.from_np(a.dtype), kind="ExternalInput").ap()
    out = nc.dram_tensor("out_rows", [NODES, D], F32, kind="ExternalOutput").ap()
    build(nc, args["x"], *(args[n] for n in _EDGE), args, out)
    r = _run(nc, [arrays], core_ids=[0])
    return r.results[0]["out_rows"]
```
